# Optimizing a Trainium2 kernel written in Bass

```python
import numpy as np
import jax
import jax.numpy as jnp

def _softmax(x, axis=-1):
    return jax.nn.softmax(x, axis=axis)

def _gelu(x):
    return jax.nn.gelu(x, approximate=True)

def _silu(x):
    return jax.nn.silu(x)

def _sigmoid(x):
    return jax.nn.sigmoid(x)

def _layernorm(x, axis=-1, eps=1e-05):
    m = jnp.mean(x, axis=axis, keepdims=True)
    v = jnp.var(x, axis=axis, keepdims=True)
    return (x - m) / jnp.sqrt(v + eps)

def _scatter_add(tgt, idx, src, axis=0):
    return tgt.at[idx].add(src)

def _segment_sum(src, seg, n):
    return jax.ops.segment_sum(src, seg, n)
kernel_name = 'mk_gnn_preln_d2_gnn_r64_0bffca'

def setup_inputs(seed: int=0):
    np.random.seed(seed)
    _w = jnp.asarray

    def _rec_inputs():
        import jax
        import jax.numpy as jnp
        _gk = jax.random.key(seed)
        x = -0.0002117 + 1 * jax.random.normal(jax.random.fold_in(_gk, 1), (100000, 256), jnp.float32)
        src = jax.random.randint(jax.random.fold_in(_gk, 2), (25000,), 0, 100000, jnp.int32)
        dst = jax.random.randint(jax.random.fold_in(_gk, 3), (25000,), 0, 100000, jnp.int32)
        _o = jnp.argsort(dst, stable=True)
        src = src[_o]
        dst = dst[_o]
        edge_weight = jax.random.uniform(jax.random.fold_in(_gk, 14), (25000,), jnp.float32, 0.0, 1)
        return (x, src, dst, edge_weight)
    x, src, dst, edge_weight = _rec_inputs()

    def _L0_gnn_setup():
        import jax, jax.numpy as jnp
        import numpy as np
        N = 100000
        E = 50000
        D = 256
        key = jax.random.key(seed)
        ks = jax.random.split(key, 6)
        x = jax.random.normal(ks[0], (N, D), dtype=jnp.float32)
        row = jax.random.randint(ks[1], (E,), 0, N, dtype=jnp.int32)
        col = jax.random.randint(ks[2], (E,), 0, N, dtype=jnp.int32)
        values = jax.random.uniform(ks[3], (E,), dtype=jnp.float32)
        out_norm = jax.random.uniform(ks[4], (N, 1), dtype=jnp.float32)
        in_norm = jax.random.uniform(ks[5], (N, 1), dtype=jnp.float32)
        return {'x': x, 'row': row, 'col': col, 'values': values, 'out_norm': out_norm, 'in_norm': in_norm}
    _L0_gnn_all = _L0_gnn_setup()
    _L0_gnn_in = {k: v for k, v in _L0_gnn_all.items() if k in ()}
    del _L0_gnn_all

    def _L1_gnn_setup():
        import jax, jax.numpy as jnp
        import numpy as np
        N_NODES = 256
        D_FEAT = 256
        N_EDGES = 4096
        HIDDEN = 512
        D_OUT = 256
        key = jax.random.key(seed)
        ks = jax.random.split(key, 5)
        x = jax.random.normal(ks[0], (N_NODES, D_FEAT), dtype=jnp.float32)
        W1 = jax.random.normal(ks[1], (2 * D_FEAT, HIDDEN), dtype=jnp.float32) * (1.0 / np.sqrt(2 * D_FEAT))
        b1 = jnp.zeros((HIDDEN,), dtype=jnp.float32)
        W2 = jax.random.normal(ks[2], (HIDDEN, D_OUT), dtype=jnp.float32) * (1.0 / np.sqrt(HIDDEN))
        b2 = jnp.zeros((D_OUT,), dtype=jnp.float32)
        nn_index = jax.random.randint(ks[3], (2, N_EDGES), 0, N_NODES, dtype=jnp.int64)
        return {'x': x, 'W1': W1, 'b1': b1, 'W2': W2, 'b2': b2, 'nn_index': nn_index, 'k': 16}
    _L1_gnn_all = _L1_gnn_setup()
    _L1_gnn_in = {k: v for k, v in _L1_gnn_all.items() if k in ('W1', 'b1', 'W2', 'b2')}
    del _L1_gnn_all
    return {'x': x, 'src': src, 'dst': dst, 'edge_weight': edge_weight, 'L1_gnn_W1': _L1_gnn_in['W1'], 'L1_gnn_b1': _L1_gnn_in['b1'], 'L1_gnn_W2': _L1_gnn_in['W2'], 'L1_gnn_b2': _L1_gnn_in['b2']}

def reference(x, src, dst, edge_weight, L1_gnn_W1, L1_gnn_b1, L1_gnn_W2, L1_gnn_b2):
    import jax
    import jax.numpy as jnp

    def _L0_gnn_ref(x, row, col, values, out_norm, in_norm):
        import jax, jax.numpy as jnp
        import numpy as np
        N = 100000
        E = 50000
        D = 256
        xs = out_norm * x
        msg = xs[col] * values[:, None]
        agg = jax.ops.segment_sum(msg, row, num_segments=N)
        return in_norm * agg

    def _L1_gnn_ref(x, W1, b1, W2, b2, nn_index, k):
        import jax, jax.numpy as jnp
        import numpy as np
        N_NODES = 256
        D_FEAT = 256
        N_EDGES = 4096
        HIDDEN = 512
        D_OUT = 256
        num_nodes = x.shape[0]
        src = nn_index[0]
        tgt = nn_index[1]
        x_i = x[tgt]
        x_j = x[src]
        feat = jnp.concatenate([x_i, x_j - x_i], axis=-1)
        h = jax.nn.relu(feat @ W1 + b1)
        msg = h @ W2 + b2
        out = jax.ops.segment_sum(msg, tgt, num_segments=num_nodes)
        deg = jax.ops.segment_sum(jnp.ones((msg.shape[0], 1), dtype=msg.dtype), tgt, num_segments=num_nodes)
        return out / (deg + 1e-08)
    edge_index = jnp.stack([src, dst])
    deg = jnp.maximum(jax.ops.segment_sum(jnp.ones(dst.shape, jnp.float32), dst, num_segments=100000), 1.0)
    deg_isqrt = deg ** (-0.5)
    h = jnp.maximum(_layernorm(x, axis=-1), 0.0)
    x = x + _L0_gnn_ref(h, src, dst, edge_weight, deg_isqrt[:, None], deg_isqrt[:, None])
    h = jnp.maximum(_layernorm(x, axis=-1), 0.0)
    x = x + _L1_gnn_ref(h, L1_gnn_W1, L1_gnn_b1, L1_gnn_W2, L1_gnn_b2, edge_index, 16)
    return x

_drawn_inputs = setup_inputs


def setup_inputs(seed=0):
    import zlib

    import numpy as np

    out = dict(_drawn_inputs(seed))
    spreads = {'L1_gnn_b1': (0.0, 0.1), 'L1_gnn_b2': (0.0, 0.1)}
    factors = {}
    for name, (base, spread) in spreads.items():
        noise = np.random.default_rng([zlib.crc32(name.encode()), seed]).standard_normal(out[name].shape)
        drawn = base * np.exp(spread * noise) if base else spread * noise
        out[name] = jnp.asarray(drawn.astype(out[name].dtype))
    for name, factor in factors.items():
        out[name] = (out[name] * factor).astype(out[name].dtype)
    return out
```

```python
import concourse.bass as bass
from concourse import mybir
from contextlib import ExitStack


def gnn_preln_two_layers(nc, x, src, dst, edge_weight, w1, b1, w2, b2, out):
    fp32 = mybir.dt.float32
    fp32r = mybir.dt.float32r
    bf16 = mybir.dt.bfloat16
    fp16 = mybir.dt.float16
    i32 = mybir.dt.int32
    ALU = mybir.AluOpType
    ACT = mybir.ActivationFunctionType
    AX = mybir.AxisListType

    P = 128
    N, D = x.shape
    E = src.shape[0]
    HID = w1.shape[1]
    EP = 125
    T = E // EP
    assert EP * T == E
    W = 4
    NB = T // W
    HALF = NB // 2
    G = 2
    ROWS = out.shape[0]
    SPARE = N
    PADKEY = N + W * P
    LO = 128
    C = (PADKEY + P - 1) // LO // P + 1
    KF = 2 * D // P
    KD = D // P
    KH = HID // P
    CW = D + W
    EPS = 1e-5

    BULK = 100
    FLIGHT = 4
    x_flat = x.rearrange("n d -> (n d)").rearrange("(c a w) -> c a w", c=BULK, a=16)
    x1_d = nc.dram_tensor("x1", (ROWS, D), fp32).ap()
    x1_head = x1_d[0:N, :].rearrange("n d -> (n d)").rearrange("(c a w) -> c a w", c=BULK, a=16)
    x1_flat = x1_d.rearrange("n d -> (n d)").rearrange("(c a w) -> c a w", c=BULK, a=16)
    out_flat = out.rearrange("n d -> (n d)").rearrange("(c a w) -> c a w", c=BULK, a=16)
    ZR = ROWS - N
    spare_rows = x1_d[N:ROWS, :].rearrange("(p a) d -> p (a d)", p=100)
    PREP_ROUNDS = 25
    PER_BATCH0 = 4
    BULK_BATCHES0 = (BULK - PREP_ROUNDS * FLIGHT) // PER_BATCH0
    PER_BATCH1 = 4
    BULK_BATCHES1 = BULK // PER_BATCH1
    assert PREP_ROUNDS * FLIGHT + BULK_BATCHES0 * PER_BATCH0 == BULK
    assert BULK_BATCHES1 * PER_BATCH1 == BULK

    src_rows_d = nc.dram_tensor("src_rows", (T, P), fp32).ap()
    dst_rows_d = nc.dram_tensor("dst_rows", (T, P), fp32).ap()
    hi_rows_d = nc.dram_tensor("hi_rows", (2, T, P), fp16).ap()
    src_rows = src_rows_d.rearrange("(b j) p -> b (j p)", j=W)
    dst_rows = dst_rows_d.rearrange("(b j) p -> b (j p)", j=W)
    hi_rows = hi_rows_d.rearrange("k (b j) p -> b k (j p)", j=W)

    ctx = ExitStack()
    with ctx:
        def sb(name, shape, dt):
            return ctx.enter_context(nc.sbuf_tensor(name, shape, dt))

        def sem(name):
            return ctx.enter_context(nc.semaphore(name))

        keys = sb("keys", [P, 2, T], i32)
        row_idx = sb("row_idx", [P, T], i32)
        weight = sb("weight", [P, T], fp32)
        K_SRC, K_DST, K_SLO, K_DLO, K_VAL = range(5)
        per_edge = sb("per_edge", [P, NB, 5, W], fp32)
        degree = sb("degree", [P, NB, W], fp32)
        eps_col = sb("eps_col", [P, 1], fp32)
        ident = sb("ident", [P, P], fp32)
        hi_ident = sb("hi_ident", [P, C], fp32)
        lo_iota = sb("lo_iota", [P, LO], fp32)
        later = sb("later", [P, P], fp32)
        later_tile = sb("later_tile", [P, W, W], fp32)
        spare = sb("spare", [P, W], fp32)
        table = sb("table", [P, C, 2, LO], bf16)
        b1_col = sb("b1_col", [P, KH], fp32)
        b2_row = sb("b2_row", [P, D], fp32)
        w1_hi = sb("w1_hi", [P, KF, HID], fp32r)
        w1_lo = sb("w1_lo", [P, KF, HID], fp32r)
        w2_hi = sb("w2_hi", [P, KH, D], fp32r)
        w2_lo = sb("w2_lo", [P, KH, D], fp32r)
        waited = sem("waited")

        bulk = [sem(f"bulk{k}") for k in range(FLIGHT)]
        bulk_out = [sem(f"bulk_out{k}") for k in range(FLIGHT)]

        with ExitStack() as stage:
            def sb(name, shape, dt):
                return stage.enter_context(nc.sbuf_tensor(name, shape, dt))

            def pb(name, shape, dt):
                return stage.enter_context(nc.psum_tensor(name, shape, dt))

            keys_f = sb("keys_f", [P, 2, T], fp32)
            hi_i = sb("hi_i", [P, 2, T], i32)
            lo_i = sb("lo_i", [P, 2, T], i32)
            hi_f = sb("hi_f", [P, 2, T], fp32)
            rows_f = sb("rows_f", [P, 2, 2, P], fp32)
            rows_h = sb("rows_h", [P, 2, 2, P], fp16)
            w1_f = sb("w1_f", [P, KF, HID], fp32)
            w2_f = sb("w2_f", [P, KH, D], fp32)
            wd = sb("wd", [P, KD, HID], fp32)
            b1_f = sb("b1_f", [KH, P], fp32)
            zero_rows = sb("zero_rows", [100, ZR * D // 100], fp32)
            zero_bf = sb("zero_bf", [P, 512], bf16)
            hi_iota_i = sb("hi_iota_i", [P, C * P], i32)
            hi_iota = sb("hi_iota", [P, C * P], fp16)
            lo_iota_i = sb("lo_iota_i", [P, LO], i32)
            lo_iota_h = sb("lo_iota_h", [P, LO], fp16)
            hi_ident_i = sb("hi_ident_i", [P, C], i32)
            part_i = sb("part_i", [P, W + 1], i32)
            part_f = sb("part_f", [P, W + 1], fp32)
            hot_hi = sb("hot_hi", [P, W, C * P], bf16)
            hot_lo = sb("hot_lo", [P, W, LO], bf16)
            node_count = sb("node_count", [P, C * P], fp32)
            table_i = sb("table_i", [P, C, LO], i32)
            table_r = sb("table_r", [P, C, LO], i32)
            table_rf = sb("table_rf", [P, C, LO], fp32)
            table_f = sb("table_f", [P, C, LO], fp32)
            CH = C * P // 2
            ps_count = [pb(f"ps_count{h}", [P, 512], fp32) for h in range(2)]
            ps_tab = [pb(f"ps_tab{h}", [P, 512], fp32) for h in range(2)]
            ps_rows = [pb(f"ps_rows{h}", [P, 512], fp32) for h in range(2)]
            ps_b1 = pb("ps_b1", [P, 512], fp32)

            padded = sem("padded")
            consts = sem("consts")
            ident_zero = sem("ident_zero")
            edges_in = sem("edges_in")
            weights_in = sem("weights_in")
            split_keys = sem("split_keys")
            hots_ready = sem("hots_ready")
            hots_free = sem("hots_free")
            counted = sem("counted")
            copied = sem("copied")
            tabled = sem("tabled")
            tab_steps = sem("tab_steps")
            w_steps = sem("w_steps")
            rows_turned = sem("rows_turned")
            rows_copied = sem("rows_copied")
            rows_out = sem("rows_out")
            b1_turned = sem("b1_turned")
            zeroed = sem("zeroed")
            idents_made = sem("idents_made")

            block = stage.enter_context(nc.Block())

            @block.sync
            def _(sp):
                sp.wait_ge(padded, 3)
                sp.dma_start(keys[0:EP, 0, :], src.rearrange("(p t) -> p t", t=T)).then_inc(edges_in, 16)
                sp.dma_start(keys[0:EP, 1, :], dst.rearrange("(p t) -> p t", t=T)).then_inc(edges_in, 16)
                sp.dma_start(weight[0:EP, :], edge_weight.rearrange("(p t) -> p t", t=T)).then_inc(edges_in, 16)
                sp.dma_start(w1_f[:], w1.rearrange("(k p) h -> p k h", p=P)).then_inc(weights_in, 16)
                sp.dma_start(w2_f[:], w2.rearrange("(k p) d -> p k d", p=P)).then_inc(weights_in, 16)
                sp.dma_start(b1_f[:], b1.rearrange("(k p) -> k p", p=P)).then_inc(weights_in, 16)
                sp.dma_start(b2_row[:], b2.partition_broadcast(P)).then_inc(weights_in, 16)
                sp.wait_ge(zeroed, 1)
                sp.dma_start(spare_rows, zero_rows[:]).then_inc(rows_out, 16)
                for k in range(FLIGHT):
                    sp.dma_start(x1_head[k], x_flat[k]).then_inc(bulk[k], 16)
                with sp.Fori(1, PREP_ROUNDS) as r:
                    for k in range(FLIGHT):
                        sp.wait_ge(bulk[k], 16 * r)
                        sp.dma_start(x1_head[bass.ds(FLIGHT * r + k, 1)],
                                     x_flat[bass.ds(FLIGHT * r + k, 1)]).then_inc(bulk[k], 16)
                sp.wait_ge(rows_copied, 2)
                for half, (t0, n) in enumerate(((0, P), (P, T - P))):
                    sp.dma_start(src_rows_d[t0:t0 + n, :], rows_f[0:n, 0, half, :]).then_inc(rows_out, 16)
                    sp.dma_start(dst_rows_d[t0:t0 + n, :], rows_f[0:n, 1, half, :]).then_inc(rows_out, 16)
                    for key in range(2):
                        sp.dma_start(hi_rows_d[key, t0:t0 + n, :],
                                     rows_h[0:n, key, half, :]).then_inc(rows_out, 16)
                sp.wait_ge(rows_out, 16 * 9)

            @block.gpsimd
            def _(pool):
                for key in range(2):
                    nc.gpsimd.iota(keys[:, key, :], [[0, T]], base=PADKEY, channel_multiplier=1).then_inc(padded, 1)
                nc.gpsimd.memset(weight[:], 0.0).then_inc(padded, 1)
                nc.gpsimd.memset(zero_rows[:], 0.0).then_inc(zeroed, 1)
                nc.gpsimd.memset(ident[:], 0.0).then_inc(ident_zero, 1)
                pool.wait_ge(ident_zero, 1)
                nc.gpsimd.affine_select(out=ident[:], in_=ident[:], compare_op=ALU.not_equal, fill=1.0,
                                        base=0, pattern=[[-1, P]], channel_multiplier=1).then_inc(idents_made, 1)
                nc.gpsimd.iota(hi_iota_i[:], [[1, C * P]], base=0, channel_multiplier=0).then_inc(consts, 1)
                nc.gpsimd.iota(lo_iota_i[:], [[1, LO]], base=0, channel_multiplier=0).then_inc(consts, 1)
                nc.gpsimd.iota(hi_ident_i[:], [[P, C]], base=0, channel_multiplier=1).then_inc(consts, 1)
                nc.gpsimd.iota(part_i[:, 0:W], [[P, W]], base=SPARE, channel_multiplier=1).then_inc(consts, 1)
                nc.gpsimd.iota(part_i[:, W:W + 1], [[0, 1]], base=0, channel_multiplier=1).then_inc(consts, 1)

            @block.vector
            def _(dve):
                nc.vector.memset(zero_bf[:], 0.0).then_inc(copied, 1)
                nc.vector.memset(eps_col[:], EPS)
                nc.vector.memset(later_tile[:], 0.0).then_inc(tab_steps, 1)
                dve.wait_ge(tab_steps, 1)
                for a in range(W - 1):
                    nc.vector.memset(later_tile[:, a, a + 1:W], 1.0)
                dve.wait_ge(consts, 5)
                nc.vector.tensor_copy(hi_iota[:], hi_iota_i[:])
                nc.vector.tensor_copy(lo_iota[:], lo_iota_i[:])
                nc.vector.tensor_copy(lo_iota_h[:], lo_iota_i[:])
                nc.vector.tensor_copy(hi_ident[:], hi_ident_i[:])
                nc.vector.tensor_copy(part_f[:], part_i[:]).then_inc(tab_steps, 1)
                dve.wait_ge(tab_steps, 2)
                nc.vector.tensor_copy(spare[:], part_f[:, 0:W])
                nc.vector.tensor_scalar(later[:], lo_iota[:], part_f[:, W:W + 1], None, ALU.is_gt)
                dve.wait_ge(edges_in, 48)
                nc.vector.tensor_scalar(hi_i[:], keys[:], 7, None, ALU.logical_shift_right)
                nc.vector.tensor_scalar(lo_i[:], keys[:], LO - 1, None, ALU.bitwise_and)
                nc.vector.tensor_copy(keys_f[:], keys[:])
                nc.vector.tensor_scalar(row_idx[:], keys[:, 1, :], float(N - 1), None, ALU.min).then_inc(split_keys, 1)
                dve.wait_ge(split_keys, 1)
                nc.vector.tensor_copy(hi_f[:], hi_i[:])
                for kind, what in ((K_SRC, keys_f[:, 0, :]), (K_DST, keys_f[:, 1, :]), (K_SLO, lo_i[:, 0, :]),
                                   (K_DLO, lo_i[:, 1, :]), (K_VAL, weight[:])):
                    nc.vector.tensor_copy(per_edge[:, :, kind, :], what.rearrange("p (b j) -> p b j", j=W))\
                        .then_inc(split_keys, 1)
                dve.wait_ge(split_keys, 6)
                with dve.Fori(0, NB) as b:
                    for j in range(W):
                        dve.wait_ge(hots_free, W * b + j + 1)
                        nc.vector.tensor_scalar(hot_lo[:, j, :], lo_iota_h[:], per_edge[:, bass.ds(b, 1), K_DLO, j:j + 1],
                                                None, ALU.is_equal)
                        nc.vector.tensor_scalar(hot_hi[:, j, :], hi_iota[:], hi_f[:, 1, bass.ds(W * b + j, 1)],
                                                None, ALU.is_equal).then_inc(hots_ready, 1)
                dve.wait_ge(rows_turned, 1)
                for h, n in enumerate((P, T - P)):
                    for key in range(2):
                        at = (2 * h + key) * P
                        nc.vector.tensor_copy(rows_f[0:n, key, h, :], ps_rows[0][0:n, at:at + P])
                        last = nc.vector.tensor_copy(rows_h[0:n, key, h, :], ps_rows[1][0:n, at:at + P])
                last.then_inc(rows_copied, 2)
                dve.wait_ge(b1_turned, 1)
                nc.vector.tensor_copy(b1_col[:], ps_b1[:, 0:KH])
                dve.wait_ge(counted, 1)
                for h in range(2):
                    last = nc.vector.tensor_copy(node_count[:, h * CH:(h + 1) * CH], ps_count[h][:, 0:CH])
                last.then_inc(copied, 1)
                dve.wait_ge(tabled, 1)
                for c in range(C):
                    last = nc.vector.tensor_copy(table_i[:, c, :], ps_tab[c // 4][:, (c % 4) * P:(c % 4 + 1) * P])
                last.then_inc(tab_steps, 1)
                dve.wait_ge(tab_steps, 3)
                nc.vector.tensor_scalar(table_r[:], table_i[:], 255, None, ALU.bitwise_and)
                nc.vector.tensor_copy(table_f[:], table_i[:]).then_inc(tab_steps, 1)
                dve.wait_ge(tab_steps, 4)
                nc.vector.tensor_copy(table_rf[:], table_r[:]).then_inc(tab_steps, 1)
                dve.wait_ge(tab_steps, 5)
                nc.vector.tensor_copy(table[:, :, 1, :], table_rf[:])
                nc.vector.tensor_tensor(table[:, :, 0, :], table_f[:], table_rf[:], ALU.subtract)
                dve.wait_ge(weights_in, 64)
                nc.vector.tensor_tensor(wd[:], w1_f[:, 0:KD, :], w1_f[:, KD:KF, :], ALU.subtract).then_inc(w_steps, 1)
                dve.wait_ge(w_steps, 1)
                nc.vector.tensor_copy(w1_hi[:, 0:KD, :], wd[:])
                nc.vector.tensor_copy(w1_hi[:, KD:KF, :], w1_f[:, KD:KF, :])
                nc.vector.tensor_copy(w2_hi[:], w2_f[:]).then_inc(w_steps, 1)
                dve.wait_ge(w_steps, 2)
                nc.vector.tensor_tensor(w1_lo[:, 0:KD, :], wd[:], w1_hi[:, 0:KD, :].bitcast(fp32), ALU.subtract)
                nc.vector.tensor_tensor(w1_lo[:, KD:KF, :], w1_f[:, KD:KF, :],
                                        w1_hi[:, KD:KF, :].bitcast(fp32), ALU.subtract)
                nc.vector.tensor_tensor(w2_lo[:], w2_f[:], w2_hi[:].bitcast(fp32), ALU.subtract)

            @block.tensor
            def _(pe):
                pe.wait_ge(copied, 1)
                for h in range(2):
                    nc.tensor.matmul(ps_count[h][:, 0:CH], zero_bf[:, 0:P], zero_bf[:, 0:CH], start=True, stop=False)
                pe.sem_inc(hots_free, W)
                with pe.Fori(0, NB) as b:
                    for j in range(W):
                        pe.wait_ge(hots_ready, W * b + j + 1)
                        for h in range(2):
                            last = nc.tensor.matmul(ps_count[h][:, 0:CH], hot_lo[:, j, :],
                                                    hot_hi[:, j, h * CH:(h + 1) * CH], start=False, stop=False)
                        last.then_inc(hots_free, 1)
                for h in range(2):
                    last = nc.tensor.matmul(ps_count[h][:, 0:CH], zero_bf[:, 0:P], zero_bf[:, 0:CH],
                                            start=False, stop=True)
                last.then_inc(counted, 1)
                pe.wait_ge(idents_made, 1)
                for w, what in enumerate((keys_f, hi_f)):
                    for half, (t0, n) in enumerate(((0, P), (P, T - P))):
                        for key in range(2):
                            at = (2 * half + key) * P
                            last = nc.tensor.transpose(ps_rows[w][0:n, at:at + P], what[:, key, t0:t0 + n], ident[:])
                last.then_inc(rows_turned, 1)
                pe.wait_ge(weights_in, 64)
                nc.tensor.transpose(ps_b1[:, 0:KH], b1_f[:], ident[0:KH, 0:KH]).then_inc(b1_turned, 1)
                pe.wait_ge(copied, 2)
                for c in range(C):
                    last = nc.tensor.transpose(ps_tab[c // 4][:, (c % 4) * P:(c % 4 + 1) * P],
                                               node_count[:, c * P:(c + 1) * P], ident[:])
                last.then_inc(tabled, 1)

        with ExitStack() as stage:
            def sb(name, shape, dt):
                return stage.enter_context(nc.sbuf_tensor(name, shape, dt))

            def pb(name, shape, dt):
                return stage.enter_context(nc.psum_tensor(name, shape, dt))

            gather_idx = [sb(f"gather_idx{q}", [P, W], i32) for q in range(2)]
            rows = [sb(f"rows{q}", [P, W, D], fp32) for q in range(2)]
            src_row = [sb(f"src_row{q}", [P, W * P], fp32) for q in range(2)]
            hi_row = [sb(f"hi_row{q}", [P, 2, W * P], fp16) for q in range(2)]
            cols = [sb(f"cols{q}", [P, 5, W], fp32) for q in range(2)]
            moments = sb("moments", [P, W, 6], fp32)
            mean_var = [sb(f"mean_var{q}", [P, W, 2], fp32) for q in range(2)]
            std = sb("std", [P, W], fp32)
            rstd = [sb(f"rstd{q}", [P, W], fp32) for q in range(2)]
            shift = [sb(f"shift{q}", [P, W], fp32) for q in range(2)]
            normed = [sb(f"normed{q}", [P, W, D], fp32) for q in range(2)]
            hot = [sb(f"hot{k}", [P, C, W * P], bf16) for k in range(2)]
            picked = sb("picked", [P, 2, W, LO], bf16)
            deg = [sb(f"deg{q}", [P, 2, W], fp32) for q in range(2)]
            deg_max = sb("deg_max", [P, W], fp32)
            deg_prod = sb("deg_prod", [P, W], fp32)
            root = sb("root", [P, W], fp32)
            inv_root = sb("inv_root", [P, W], fp32)
            coef = [sb(f"coef{q}", [P, W], fp32) for q in range(2)]
            same = sb("same", [P, W, W * P], fp32r)
            same_later = sb("same_later", [P, W, P], fp32)
            dup_in = [sb(f"dup_in{q}", [P, W], fp32) for q in range(2)]
            msg_hi = sb("msg_hi", [P, W, CW], fp32r)
            msg_lo = sb("msg_lo", [P, W, D], fp32r)
            stage_rows = [sb(f"stage_rows{q}", [P, W, CW], fp32) for q in range(2)]
            dup_tile = sb("dup_tile", [P, W, W], fp32)
            dup = sb("dup", [P, W], fp32)
            dup_all = sb("dup_all", [P, W], fp32)
            is_dup = sb("is_dup", [P, W], fp32)
            to_spare = sb("to_spare", [P, W], fp32)
            move = sb("move", [P, W], fp32)
            scatter_f = sb("scatter_f", [P, W], fp32)
            scatter_idx = [sb(f"scatter_idx{q}", [P, W], i32) for q in range(2)]
            ps_deg = [pb(f"ps_deg{k}", [P, W * P], fp32) for k in range(2)]
            ps_sum = [pb(f"ps_sum{a}", [P, 512], fp32) for a in range(W)]

            rows_in = [sem(f"rows_in{q}") for q in range(2)]
            keys_in = [sem(f"keys_in{q}") for q in range(2)]
            keyrows_free = sem("keyrows_free")
            idx_staged = sem("idx_staged")
            moments_done = sem("moments_done")
            var_done = sem("var_done")
            std_done = sem("std_done")
            rstd_done = sem("rstd_done")
            shift_done = sem("shift_done")
            normed_done = sem("normed_done")
            hot_ready = sem("hot_ready")
            deg_ready = sem("deg_ready")
            cols_ready = sem("cols_ready")
            same_ready = sem("same_ready")
            same_later_done = sem("same_later_done")
            dup_in_done = sem("dup_in_done")
            deg_picked = sem("deg_picked")
            coef_steps = sem("coef_steps")
            root_done = sem("root_done")
            coef_ready = sem("coef_ready")
            hi_ready = sem("hi_ready")
            lo_ready = sem("lo_ready")
            summed = sem("summed")
            staged = sem("staged")
            stage_free = sem("stage_free")
            idx_steps = sem("idx_steps")
            idx_ready = sem("idx_ready")
            scattered = sem("scattered")
            cnt_cols = sem("cnt_cols")

            block = stage.enter_context(nc.Block())

            @block.sync
            def _(sp):
                def load(b, i, q):
                    sp.wait_ge(keyrows_free, b + 1)
                    sp.dma_start(src_row[q][:], src_rows[bass.ds(b, 1), :].partition_broadcast(P))\
                        .then_inc(keys_in[q], 16)
                    sp.dma_start(hi_row[q][:], hi_rows[bass.ds(b, 1), :, :].partition_broadcast(P))\
                        .then_inc(keys_in[q], 16)

                def copy_on(b):
                    for k in range(PER_BATCH0):
                        sp.wait_ge(bulk[k], 16 * (b + PREP_ROUNDS))
                        sp.dma_start(x1_head[bass.ds(FLIGHT * (b + PREP_ROUNDS) + k, 1)],
                                     x_flat[bass.ds(FLIGHT * (b + PREP_ROUNDS) + k, 1)]).then_inc(bulk[k], 16)

                with sp.Fori(0, HALF) as i:
                    for q in range(2):
                        load(2 * i + q, i, q)

            @block.gpsimd
            def _(pool):
                nc.gpsimd.memset(msg_hi[:, :, D:CW].bitcast(fp32), 0.0).then_inc(cnt_cols, 1)
                pool.wait_ge(cnt_cols, 1)
                for j in range(W):
                    nc.gpsimd.memset(msg_hi[:, j, D + j:D + j + 1].bitcast(fp32), 1.0).then_inc(cnt_cols, 1)

                def gather(b, i, q):
                    pool.wait_ge(normed_done, b + 1)
                    pool.sem_inc(waited, 1)
                    nc.gpsimd.tensor_copy(gather_idx[q][:], row_idx[:, bass.ds(W * b, W)]).then_inc(idx_staged, 1)
                    pool.wait_ge(idx_staged, b + 1)
                    pool.sem_inc(waited, 1)
                    for j in range(W):
                        pool.indirect_dma_start(
                            out=rows[q][:, j, :], out_offset=None, in_=x,
                            in_offset=bass.IndirectOffsetOnAxis(ap=gather_idx[q][:, j:j + 1], axis=0))\
                            .then_inc(rows_in[q], 16)

                def scatter(b, i, q):
                    pool.wait_ge(staged, b + 1)
                    pool.wait_ge(idx_ready, b + 1)
                    pool.sem_inc(waited, 1)
                    for j in range(W):
                        pool.indirect_dma_start(
                            out=x1_d, out_offset=bass.IndirectOffsetOnAxis(ap=scatter_idx[q][:, j:j + 1], axis=0),
                            in_=stage_rows[q][:, j, 0:D], in_offset=None, compute_op=ALU.add)\
                            .then_inc(scattered, 16)

                def scatter_end(b):
                    pool.wait_ge(scattered, 16 * W * (b + 1))
                    pool.sem_inc(stage_free, 1)

                gather(0, 0, 0)
                gather(1, 0, 1)
                for k in range(FLIGHT):
                    pool.wait_ge(bulk[k], 16 * (BULK // FLIGHT))
                with pool.Fori(0, HALF - 1) as i:
                    for q in range(2):
                        scatter(2 * i + q, i, q)
                        gather(2 * i + 2 + q, i + 1, q)
                        scatter_end(2 * i + q)
                for q in range(2):
                    scatter(NB - 2 + q, HALF - 1, q)
                    scatter_end(NB - 2 + q)

            @block.vector
            def _(dve):
                dve.sem_inc(keyrows_free, 2)

                def build(b, i, q):
                    dve.wait_ge(rows_in[q], 16 * W * (i + 1))
                    for j in range(W):
                        last = nc.vector.bn_stats(moments[:, j, :], rows[q][:, j, :])
                    last.then_inc(moments_done, 1)
                    dve.wait_ge(moments_done, b + 1)
                    dve.sem_inc(waited, 1)
                    for j in range(W):
                        last = nc.vector.bn_aggr(mean_var[q][:, j, :], moments[:, j, :])
                    last.then_inc(var_done, 1)
                    dve.wait_ge(keys_in[q], 32 * (i + 1))
                    for k in range(2):
                        dve.wait_ge(deg_ready, 2 * b + k + 1)
                        for c in range(C):
                            last = nc.vector.tensor_scalar(hot[k][:, c, :], hi_row[q][:, k, :], hi_ident[:, c:c + 1],
                                                           None, ALU.is_equal)
                        last.then_inc(hot_ready, 1)
                    nc.vector.tensor_copy(cols[q][:], per_edge[:, bass.ds(b, 1), :, :]).then_inc(cols_ready, 1)
                    dve.wait_ge(std_done, b + 1)
                    nc.vector.reciprocal(rstd[q][:], std[:]).then_inc(rstd_done, 1)
                    dve.wait_ge(rstd_done, b + 1)
                    nc.vector.scalar_tensor_tensor(shift[q][:], mean_var[q][:, :, 0], -1.0, rstd[q][:],
                                                   ALU.mult, ALU.mult).then_inc(shift_done, 1)
                    dve.wait_ge(cols_ready, b + 1)
                    dve.wait_ge(summed, b + 1)
                    for j in range(W):
                        last = nc.vector.tensor_scalar(same[:, j, :], src_row[q][:], cols[q][:, K_SRC, j:j + 1],
                                                       None, ALU.is_equal)
                    last.then_inc(same_ready, 1)
                    dve.wait_ge(same_ready, b + 1)
                    dve.sem_inc(keyrows_free, 1)
                    for j in range(W):
                        last = nc.vector.tensor_tensor(same_later[:, j, :], same[:, j, j * P:(j + 1) * P].bitcast(fp32),
                                                       later[:], ALU.mult)
                    last.then_inc(same_later_done, 1)
                    dve.wait_ge(same_later_done, b + 1)
                    nc.vector.tensor_reduce(dup_in[q][:], same_later[:], AX.X, ALU.add).then_inc(dup_in_done, 1)
                    for k, kind in enumerate((K_SLO, K_DLO)):
                        dve.wait_ge(deg_ready, 2 * b + k + 3)
                        for j in range(W):
                            last = nc.vector.scalar_tensor_tensor(
                                picked[:, k, j, :], lo_iota[:], cols[q][:, kind, j:j + 1], ps_deg[k][:, j * P:(j + 1) * P],
                                ALU.is_equal, ALU.mult, accum_out=deg[q][:, k, j:j + 1])
                        last.then_inc(deg_picked, 1)
                    dve.wait_ge(deg_picked, 2 * b + 2)
                    nc.vector.tensor_scalar(deg_max[:], deg[q][:, 1, :], 1.0, None, ALU.max).then_inc(coef_steps, 1)
                    dve.wait_ge(coef_steps, 3 * b + 1)
                    nc.vector.scalar_tensor_tensor(deg_prod[:], deg[q][:, 0, :], 1.0, deg_max[:], ALU.max, ALU.mult)\
                        .then_inc(coef_steps, 1)
                    nc.vector.tensor_copy(degree[:, bass.ds(b, 1), :], deg[q][:, 1, :])
                    dve.wait_ge(root_done, b + 1)
                    nc.vector.reciprocal(inv_root[:], root[:]).then_inc(coef_steps, 1)
                    dve.wait_ge(coef_steps, 3 * b + 3)
                    nc.vector.tensor_tensor(coef[q][:], inv_root[:], cols[q][:, K_VAL, :], ALU.mult)\
                        .then_inc(coef_ready, 1)
                    dve.wait_ge(coef_ready, b + 1)
                    dve.wait_ge(hi_ready, b + 1)
                    for j in range(W):
                        last = nc.vector.scalar_tensor_tensor(
                            msg_lo[:, j, :], normed[q][:, j, :], coef[q][:, j:j + 1],
                            msg_hi[:, j, 0:D].bitcast(fp32), ALU.mult, ALU.subtract)
                    last.then_inc(lo_ready, 1)

                def targets(b, i, q):
                    dve.wait_ge(staged, b + 1)
                    dve.wait_ge(dup_in_done, b + 1)
                    nc.vector.tensor_tensor(dup_tile[:], stage_rows[q][:, :, D:CW], later_tile[:], ALU.mult)\
                        .then_inc(idx_steps, 1)
                    nc.vector.tensor_tensor(to_spare[:], spare[:], cols[q][:, K_SRC, :], ALU.subtract)
                    dve.wait_ge(idx_steps, 6 * b + 1)
                    nc.vector.tensor_reduce(dup[:], dup_tile[:], AX.X, ALU.add).then_inc(idx_steps, 1)
                    dve.wait_ge(idx_steps, 6 * b + 2)
                    nc.vector.tensor_tensor(dup_all[:], dup[:], dup_in[q][:], ALU.add).then_inc(idx_steps, 1)
                    dve.wait_ge(idx_steps, 6 * b + 3)
                    nc.vector.tensor_scalar(is_dup[:], dup_all[:], 0.5, None, ALU.is_gt).then_inc(idx_steps, 1)
                    dve.wait_ge(idx_steps, 6 * b + 4)
                    nc.vector.tensor_tensor(move[:], is_dup[:], to_spare[:], ALU.mult).then_inc(idx_steps, 1)
                    dve.wait_ge(idx_steps, 6 * b + 5)
                    nc.vector.tensor_tensor(scatter_f[:], move[:], cols[q][:, K_SRC, :], ALU.add).then_inc(idx_steps, 1)
                    dve.wait_ge(idx_steps, 6 * b + 6)
                    nc.vector.tensor_copy(scatter_idx[q][:], scatter_f[:]).then_inc(idx_ready, 1)

                build(0, 0, 0)
                with dve.Fori(0, HALF - 1) as i:
                    build(2 * i + 1, i, 1)
                    targets(2 * i, i, 0)
                    build(2 * i + 2, i + 1, 0)
                    targets(2 * i + 1, i, 1)
                build(NB - 1, HALF - 1, 1)
                targets(NB - 2, HALF - 1, 0)
                targets(NB - 1, HALF - 1, 1)

            @block.scalar
            def _(act):
                act.sem_inc(normed_done, 2)
                act.sem_inc(stage_free, 2)

                def norm(b, i, q):
                    act.wait_ge(var_done, b + 1)
                    act.wait_ge(rstd_done, b) if not isinstance(b, int) or b else None
                    nc.scalar.activation(std[:], mean_var[q][:, :, 1], ACT.Sqrt, bias=eps_col[:]).then_inc(std_done, 1)
                    act.wait_ge(shift_done, b + 1)
                    for j in range(W):
                        last = nc.scalar.activation(normed[q][:, j, :], rows[q][:, j, :], ACT.Relu,
                                                    bias=shift[q][:, j:j + 1], scale=rstd[q][:, j:j + 1])
                    last.then_inc(normed_done, 1)

                def message(b, i, q):
                    act.wait_ge(coef_steps, 3 * b + 2)
                    nc.scalar.activation(root[:], deg_prod[:], ACT.Sqrt).then_inc(root_done, 1)
                    act.wait_ge(normed_done, b + 3)
                    act.wait_ge(coef_ready, b + 1)
                    act.wait_ge(summed, b + 1)
                    for j in range(W):
                        last = nc.scalar.activation(msg_hi[:, j, 0:D], normed[q][:, j, :], ACT.Copy,
                                                    scale=coef[q][:, j:j + 1])
                    last.then_inc(hi_ready, 1)

                def stage_out(b, i, q):
                    act.wait_ge(summed, b + 2)
                    act.wait_ge(stage_free, b + 1)
                    for j in range(W):
                        last = nc.scalar.activation(stage_rows[q][:, j, :], ps_sum[j][:, 0:CW], ACT.Copy)
                    last.then_inc(staged, 1)

                norm(0, 0, 0)
                message(0, 0, 0)
                with act.Fori(0, HALF - 1) as i:
                    norm(2 * i + 1, i, 1)
                    stage_out(2 * i, i, 0)
                    message(2 * i + 1, i, 1)
                    norm(2 * i + 2, i + 1, 0)
                    stage_out(2 * i + 1, i, 1)
                    message(2 * i + 2, i + 1, 0)
                norm(NB - 1, HALF - 1, 1)
                stage_out(NB - 2, HALF - 1, 0)
                message(NB - 1, HALF - 1, 1)
                stage_out(NB - 1, HALF - 1, 1)

            @block.tensor
            def _(pe):
                pe.sem_inc(deg_ready, 2)
                pe.sem_inc(summed, 1)
                pe.wait_ge(cnt_cols, 1 + W)

                def degrees(b, i, q):
                    for k in range(2):
                        pe.wait_ge(hot_ready, 2 * b + k + 1)
                        if not isinstance(b, int) or b:
                            pe.wait_ge(deg_picked, 2 * b + k - 1)
                        for j in range(W):
                            for c in range(C):
                                for part in range(2):
                                    last = nc.tensor.matmul(ps_deg[k][:, j * P:(j + 1) * P],
                                                            hot[k][:, c, j * P:(j + 1) * P], table[:, c, part, :],
                                                            start=(c == 0 and part == 0),
                                                            stop=(c == C - 1 and part == 1))
                        last.then_inc(deg_ready, 1)

                def sums(b, i, q):
                    pe.wait_ge(same_ready, b + 1)
                    pe.wait_ge(lo_ready, b + 1)
                    if not isinstance(b, int) or b:
                        pe.wait_ge(staged, b)
                    for a in range(W):
                        for j in range(W):
                            nc.tensor.matmul(ps_sum[a][:, 0:CW], same[:, j, a * P:(a + 1) * P], msg_hi[:, j, :],
                                             start=(j == 0), stop=False)
                        for j in range(W):
                            last = nc.tensor.matmul(ps_sum[a][:, 0:D], same[:, j, a * P:(a + 1) * P], msg_lo[:, j, :],
                                                    start=False, stop=(j == W - 1))
                    last.then_inc(summed, 1)

                degrees(0, 0, 0)
                with pe.Fori(0, HALF - 1) as i:
                    sums(2 * i, i, 0)
                    degrees(2 * i + 1, i, 1)
                    sums(2 * i + 1, i, 1)
                    degrees(2 * i + 2, i + 1, 0)
                sums(NB - 2, HALF - 1, 0)
                degrees(NB - 1, HALF - 1, 1)
                sums(NB - 1, HALF - 1, 1)

        with ExitStack() as stage:
            def sb(name, shape, dt):
                return stage.enter_context(nc.sbuf_tensor(name, shape, dt))

            def pb(name, shape, dt):
                return stage.enter_context(nc.psum_tensor(name, shape, dt))

            ends_idx = [sb(f"ends_idx{q}", [P, 2, W], i32) for q in range(2)]
            ends = [sb(f"ends{q}", [P, 2 * W, D], fp32) for q in range(2)]
            dst_row = [sb(f"dst_row{q}", [P, W * P], fp32) for q in range(2)]
            e_moments = sb("e_moments", [P, 2 * W, 6], fp32)
            e_mean_var = [sb(f"e_mean_var{q}", [P, 2 * W, 2], fp32) for q in range(2)]
            e_std = sb("e_std", [P, 2 * W], fp32)
            e_rstd = [sb(f"e_rstd{q}", [P, 2 * W], fp32) for q in range(2)]
            e_shift = [sb(f"e_shift{q}", [P, 2 * W], fp32) for q in range(2)]
            e_normed = sb("e_normed", [P, 2 * W, D], fp32)
            feat_hi = sb("feat_hi", [P, KF, W * P], fp32r)
            feat_lo = sb("feat_lo", [P, KF, W * P], fp32r)
            hid = [sb(f"hid{h}", [P, W * P], fp32) for h in range(2)]
            hid_hi = sb("hid_hi", [P, KH, W * P], fp32r)
            hid_lo = sb("hid_lo", [P, KH, W * P], fp32r)
            out_hi = sb("out_hi", [P, W, D], fp32r)
            out_lo = sb("out_lo", [P, W, D], fp32r)
            dst_col = [sb(f"dst_col{q}", [P, W], fp32) for q in range(2)]
            deg_col = [sb(f"deg_col{q}", [P, W], fp32) for q in range(2)]
            deg_eps = sb("deg_eps", [P, W], fp32)
            inv_deg = [sb(f"inv_deg{q}", [P, W], fp32) for q in range(2)]
            peers = [sb(f"peers{q}", [P, W, G * P], fp32r) for q in range(2)]
            copies = [sb(f"copies{q}", [P, W], fp32) for q in range(2)]
            after = sb("after", [P, G, G * P], fp32)
            peers_after = sb("peers_after", [P, W, G * P], fp32)
            n_after = sb("n_after", [P, W], fp32)
            e_is_dup = sb("e_is_dup", [P, W], fp32)
            e_to_spare = sb("e_to_spare", [P, W], fp32)
            e_move = sb("e_move", [P, W], fp32)
            e_target = sb("e_target", [P, W], fp32)
            target_idx = [sb(f"target_idx{q}", [P, W], i32) for q in range(2)]
            with_bias = sb("with_bias", [P, W, D], fp32)
            add_rows = [sb(f"add_rows{q}", [P, W, D], fp32) for q in range(2)]
            ps_t = [pb(f"ps_t{h}", [P, W * P], fp32) for h in range(2)]
            ps_h = [pb(f"ps_h{h}", [P, W * P], fp32) for h in range(2)]
            ps_m = [pb(f"ps_m{h}", [P, G * D], fp32) for h in range(2)]
            ps_s = [pb(f"ps_s{h}", [P, G * D], fp32) for h in range(2)]

            ends_in = [sem(f"ends_in{q}") for q in range(2)]
            dst_row_in = [sem(f"dst_row_in{q}") for q in range(2)]
            dst_row_free = sem("dst_row_free")
            ends_staged = sem("ends_staged")
            e_moments_done = sem("e_moments_done")
            e_var_done = sem("e_var_done")
            e_std_done = sem("e_std_done")
            e_rstd_done = sem("e_rstd_done")
            e_shift_done = sem("e_shift_done")
            e_normed_done = sem("e_normed_done")
            turned = sem("turned")
            feat_hi_done = sem("feat_hi_done")
            feat_lo_done = sem("feat_lo_done")
            mm1_done = sem("mm1_done")
            relu_done = sem("relu_done")
            hid_hi_done = sem("hid_hi_done")
            hid_lo_done = sem("hid_lo_done")
            mm2_done = sem("mm2_done")
            out_hi_done = sem("out_hi_done")
            out_lo_done = sem("out_lo_done")
            e_cols_done = sem("e_cols_done")
            e_deg_done = sem("e_deg_done")
            inv_deg_done = sem("inv_deg_done")
            after_made = sem("after_made")
            peers_ready = sem("peers_ready")
            e_idx_steps = sem("e_idx_steps")
            target_ready = sem("target_ready")
            e_summed = sem("e_summed")
            sums_read = sem("sums_read")
            e_staged = sem("e_staged")
            e_stage_free = sem("e_stage_free")
            e_scattered = sem("e_scattered")

            GROUPS = W // G
            block = stage.enter_context(nc.Block())

            def following(b, t, q):
                return b + 1, t + q, 1 - q

            def before(b, t, q):
                return b - 1, t - 1 + q, 1 - q

            def first(b):
                return isinstance(b, int) and b == 0

            @block.sync
            def _(sp):
                def load(b, q):
                    sp.wait_ge(dst_row_free, b + 1)
                    sp.dma_start(dst_row[q][:], dst_rows[bass.ds(b, 1), :].partition_broadcast(P))\
                        .then_inc(dst_row_in[q], 16)

                def copy_on(b):
                    for k in range(PER_BATCH1):
                        sp.wait_ge(bulk_out[k], 16 * b)
                        sp.dma_start(out_flat[bass.ds(FLIGHT * b + k, 1)],
                                     x1_flat[bass.ds(FLIGHT * b + k, 1)]).then_inc(bulk_out[k], 16)

                load(0, 0)
                load(1, 1)
                for k in range(FLIGHT):
                    sp.dma_start(out_flat[k], x1_flat[k]).then_inc(bulk_out[k], 16)
                with sp.Fori(1, BULK_BATCHES1) as b:
                    copy_on(b)
                with sp.Fori(1, HALF) as t:
                    for q in range(2):
                        load(2 * t + q, q)

            @block.gpsimd
            def _(pool):
                def stage_indices(b, q):
                    pool.wait_ge(e_normed_done, b + 1)
                    pool.sem_inc(waited, 1)
                    nc.gpsimd.tensor_copy(ends_idx[q][:], keys[:, :, bass.ds(W * b, W)]).then_inc(ends_staged, 1)
                    pool.wait_ge(ends_staged, b + 1)
                    pool.sem_inc(waited, 1)

                def gather(q, end):
                    for j in range(W):
                        pool.indirect_dma_start(
                            out=ends[q][:, end * W + j, :], out_offset=None, in_=x1_d,
                            in_offset=bass.IndirectOffsetOnAxis(ap=ends_idx[q][:, 1 - end, j:j + 1], axis=0))\
                            .then_inc(ends_in[q], 16)

                def scatter(b, q, g):
                    pool.wait_ge(e_staged, GROUPS * (b + 1) + g + 1)
                    pool.wait_ge(target_ready, b + 1)
                    pool.sem_inc(waited, 1)
                    for j in range(G * g, G * g + G):
                        pool.indirect_dma_start(
                            out=out, out_offset=bass.IndirectOffsetOnAxis(ap=target_idx[q][:, j:j + 1], axis=0),
                            in_=add_rows[q][:, j, :], in_offset=None, compute_op=ALU.add)\
                            .then_inc(e_scattered, 16)

                def scatter_end(b, g):
                    pool.wait_ge(e_scattered, 16 * G * (GROUPS * b + g + 1))
                    pool.sem_inc(e_stage_free, 1)

                for b in range(4):
                    stage_indices(b, b % 2)
                    gather(b % 2, 0)
                    gather(b % 2, 1)
                for k in range(FLIGHT):
                    pool.wait_ge(bulk_out[k], 16 * (BULK // FLIGHT))
                with pool.Fori(0, HALF - 2) as t:
                    for q in range(2):
                        b = 2 * t + q
                        scatter(b, q, 0)
                        stage_indices(b + 4, q)
                        gather(q, 0)
                        scatter_end(b, 0)
                        scatter(b, q, 1)
                        gather(q, 1)
                        scatter_end(b, 1)
                for b in range(NB - 4, NB):
                    for g in range(GROUPS):
                        scatter(b, b % 2, g)
                        scatter_end(b, g)

            @block.vector
            def _(dve):
                dve.sem_inc(dst_row_free, 2)
                nc.vector.memset(after[:], 0.0).then_inc(after_made, 1)
                dve.wait_ge(after_made, 1)
                nc.vector.memset(after[:, 0, P:G * P], 1.0)
                nc.vector.tensor_copy(after[:, 0, 0:P], later[:])
                nc.vector.tensor_copy(after[:, 1, P:G * P], later[:]).then_inc(after_made, 1)
                dve.wait_ge(after_made, 2)

                def moments_of(b, t, q):
                    dve.wait_ge(ends_in[q], 16 * 2 * W * (t + 1))
                    for r in range(2 * W):
                        last = nc.vector.bn_stats(e_moments[:, r, :], ends[q][:, r, :])
                    last.then_inc(e_moments_done, 1)
                    dve.wait_ge(e_moments_done, b + 1)
                    dve.sem_inc(waited, 1)
                    for r in range(2 * W):
                        last = nc.vector.bn_aggr(e_mean_var[q][:, r, :], e_moments[:, r, :])
                    last.then_inc(e_var_done, 1)

                def scales_of(b, t, q):
                    dve.wait_ge(e_std_done, b + 1)
                    nc.vector.reciprocal(e_rstd[q][:], e_std[:]).then_inc(e_rstd_done, 1)
                    dve.wait_ge(e_rstd_done, b + 1)
                    nc.vector.scalar_tensor_tensor(e_shift[q][:], e_mean_var[q][:, :, 0], -1.0, e_rstd[q][:],
                                                   ALU.mult, ALU.mult).then_inc(e_shift_done, 1)

                def peers_of(b, t, q):
                    nc.vector.tensor_copy(dst_col[q][:], per_edge[:, bass.ds(b, 1), K_DST, :])
                    nc.vector.tensor_copy(deg_col[q][:], degree[:, bass.ds(b, 1), :]).then_inc(e_cols_done, 1)
                    dve.wait_ge(e_cols_done, b + 1)
                    nc.vector.tensor_scalar(deg_eps[:], deg_col[q][:], 1e-8, None, ALU.add).then_inc(e_deg_done, 1)
                    dve.wait_ge(dst_row_in[q], 16 * (t + 1))
                    dve.wait_ge(e_summed, GROUPS * b)
                    for j in range(W):
                        g = j // G
                        last = nc.vector.tensor_scalar(peers[q][:, j, :], dst_row[q][:, g * G * P:(g + 1) * G * P],
                                                       dst_col[q][:, j:j + 1], None, ALU.is_equal, ALU.add,
                                                       accum_out=copies[q][:, j:j + 1])
                    last.then_inc(peers_ready, 1)
                    dve.wait_ge(e_deg_done, b + 1)
                    dve.wait_ge(e_staged, GROUPS * b)
                    nc.vector.reciprocal(inv_deg[q][:], deg_eps[:]).then_inc(inv_deg_done, 1)
                    nc.vector.tensor_tensor(e_to_spare[:], spare[:], dst_col[q][:], ALU.subtract)
                    dve.wait_ge(peers_ready, b + 1)
                    dve.sem_inc(dst_row_free, 1)
                    for g in range(GROUPS):
                        last = nc.vector.tensor_tensor(peers_after[:, G * g:G * g + G, :],
                                                       peers[q][:, G * g:G * g + G, :].bitcast(fp32), after[:], ALU.mult)
                    last.then_inc(e_idx_steps, 1)
                    dve.wait_ge(e_idx_steps, 5 * b + 1)
                    nc.vector.tensor_reduce(n_after[:], peers_after[:], AX.X, ALU.add).then_inc(e_idx_steps, 1)
                    dve.wait_ge(e_idx_steps, 5 * b + 2)
                    nc.vector.tensor_scalar(e_is_dup[:], n_after[:], 0.5, None, ALU.is_gt).then_inc(e_idx_steps, 1)
                    dve.wait_ge(e_idx_steps, 5 * b + 3)
                    nc.vector.tensor_tensor(e_move[:], e_is_dup[:], e_to_spare[:], ALU.mult).then_inc(e_idx_steps, 1)
                    dve.wait_ge(e_idx_steps, 5 * b + 4)
                    nc.vector.tensor_tensor(e_target[:], e_move[:], dst_col[q][:], ALU.add).then_inc(e_idx_steps, 1)
                    dve.wait_ge(e_idx_steps, 5 * b + 5)
                    dve.wait_ge(e_stage_free, GROUPS * b + GROUPS)
                    nc.vector.tensor_copy(target_idx[q][:], e_target[:]).then_inc(target_ready, 1)

                def hid_low(b, m):
                    dve.wait_ge(hid_hi_done, KH * b + m + 1)
                    nc.vector.tensor_tensor(hid_lo[:, m, :], hid[m % 2][:], hid_hi[:, m, :].bitcast(fp32),
                                            ALU.subtract).then_inc(hid_lo_done, 1)

                def feat_low(b, k):
                    dve.wait_ge(feat_hi_done, KF * b + k + 1)
                    nc.vector.tensor_tensor(feat_lo[:, k, :], ps_t[k % 2][:], feat_hi[:, k, :].bitcast(fp32),
                                            ALU.subtract).then_inc(feat_lo_done, 1)

                def out_low(b, g):
                    dve.wait_ge(out_hi_done, GROUPS * b + g + 1)
                    nc.vector.tensor_tensor(out_lo[:, G * g:G * g + G, :].rearrange("p a d -> p (a d)"), ps_m[g][:],
                                            out_hi[:, G * g:G * g + G, :].rearrange("p a d -> p (a d)").bitcast(fp32),
                                            ALU.subtract).then_inc(out_lo_done, 1)

                def add_bias(b, q, g):
                    dve.wait_ge(e_summed, GROUPS * (b + 1) + g + 1)
                    dve.wait_ge(e_staged, GROUPS * b + g + 1)
                    for a in range(G):
                        j = G * g + a
                        last = nc.vector.scalar_tensor_tensor(with_bias[:, j, :], b2_row[:], copies[q][:, j:j + 1],
                                                              ps_s[g][:, a * D:(a + 1) * D], ALU.mult, ALU.add)
                    last.then_inc(sums_read, 1)

                def step(b, t, q, last=False):
                    if not last:
                        moments_of(*following(b, t, q))
                    hid_low(b, 0)
                    if not last:
                        scales_of(*following(b, t, q))
                    hid_low(b, 1)
                    peers_of(b, t, q)
                    hid_low(b, 2)
                    hid_low(b, 3)
                    if not last:
                        feat_low(b + 1, 0)
                        feat_low(b + 1, 1)
                    if not first(b):
                        add_bias(b - 1, 1 - q, 0)
                    out_low(b, 0)
                    if not last:
                        feat_low(b + 1, 2)
                        feat_low(b + 1, 3)
                    if not first(b):
                        add_bias(b - 1, 1 - q, 1)
                    out_low(b, 1)

                moments_of(0, 0, 0)
                scales_of(0, 0, 0)
                for k in range(KF):
                    feat_low(0, k)
                step(0, 0, 0)
                with dve.Fori(0, HALF - 1) as i:
                    step(2 * i + 1, i, 1)
                    step(2 * i + 2, i + 1, 0)
                step(NB - 1, HALF - 1, 1, last=True)
                for g in range(GROUPS):
                    add_bias(NB - 1, 1, g)

            @block.scalar
            def _(act):
                act.sem_inc(e_normed_done, 2)
                act.sem_inc(e_stage_free, 2 * GROUPS)
                act.sem_inc(e_staged, GROUPS)

                def std_of(b, t, q):
                    act.wait_ge(e_var_done, b + 1)
                    if not first(b):
                        act.wait_ge(e_rstd_done, b)
                    nc.scalar.activation(e_std[:], e_mean_var[q][:, :, 1], ACT.Sqrt, bias=eps_col[:])\
                        .then_inc(e_std_done, 1)

                def norm(b, t, q, end):
                    if end == 0:
                        act.wait_ge(e_shift_done, b + 1)
                        if not first(b):
                            act.wait_ge(turned, KF * b)
                    for r in range(end * W, end * W + W):
                        last = nc.scalar.activation(e_normed[:, r, :], ends[q][:, r, :], ACT.Relu,
                                                    bias=e_shift[q][:, r:r + 1], scale=e_rstd[q][:, r:r + 1])
                    if end:
                        last.then_inc(e_normed_done, 1)

                def feat_high(b, k):
                    act.wait_ge(turned, KF * b + k + 1)
                    nc.scalar.activation(feat_hi[:, k, :], ps_t[k % 2][:], ACT.Copy).then_inc(feat_hi_done, 1)

                def hid_high(b, m):
                    act.wait_ge(mm1_done, KH * b + m + 1)
                    if not (first(b) and m < 2):
                        act.wait_ge(hid_lo_done, KH * b + m - 1)
                    nc.scalar.activation(hid[m % 2][:], ps_h[m % 2][:], ACT.Relu, bias=b1_col[:, m:m + 1])\
                        .then_inc(relu_done, 1)
                    act.wait_ge(relu_done, KH * b + m + 1)
                    nc.scalar.activation(hid_hi[:, m, :], hid[m % 2][:], ACT.Copy).then_inc(hid_hi_done, 1)

                def out_high(b, g):
                    act.wait_ge(mm2_done, GROUPS * b + g + 1)
                    nc.scalar.activation(out_hi[:, G * g:G * g + G, :].rearrange("p a d -> p (a d)"), ps_m[g][:],
                                         ACT.Copy).then_inc(out_hi_done, 1)

                def scale(b, q, g):
                    act.wait_ge(sums_read, GROUPS * b + g + 3)
                    act.wait_ge(e_stage_free, GROUPS * b + g + 1)
                    act.wait_ge(inv_deg_done, b + 1)
                    for j in range(G * g, G * g + G):
                        last = nc.scalar.activation(add_rows[q][:, j, :], with_bias[:, j, :], ACT.Copy,
                                                    scale=inv_deg[q][:, j:j + 1])
                    last.then_inc(e_staged, 1)

                def step(b, t, q, last=False):
                    nxt = following(b, t, q)
                    hid_high(b, 0)
                    if not last:
                        std_of(*nxt)
                        norm(*nxt, 0)
                    hid_high(b, 1)
                    if not last:
                        norm(*nxt, 1)
                    hid_high(b, 2)
                    hid_high(b, 3)
                    if not last:
                        feat_high(b + 1, 0)
                        feat_high(b + 1, 1)
                    if not first(b):
                        scale(b - 1, 1 - q, 0)
                    out_high(b, 0)
                    if not last:
                        feat_high(b + 1, 2)
                        feat_high(b + 1, 3)
                    if not first(b):
                        scale(b - 1, 1 - q, 1)
                    out_high(b, 1)

                std_of(0, 0, 0)
                for end in range(2):
                    norm(0, 0, 0, end)
                for k in range(KF):
                    feat_high(0, k)
                step(0, 0, 0)
                with act.Fori(0, HALF - 1) as i:
                    step(2 * i + 1, i, 1)
                    step(2 * i + 2, i + 1, 0)
                step(NB - 1, HALF - 1, 1, last=True)
                for g in range(GROUPS):
                    scale(NB - 1, 1, g)

            @block.tensor
            def _(pe):
                pe.sem_inc(sums_read, 2)
                pe.sem_inc(e_summed, GROUPS)

                def turn(b, k):
                    if k == 0:
                        pe.wait_ge(e_normed_done, b + 3)
                    if not (first(b) and k < 2):
                        pe.wait_ge(feat_lo_done, KF * b + k - 1)
                    end, c = k // KD, k % KD
                    for j in range(W):
                        last = nc.tensor.transpose(ps_t[k % 2][:, j * P:(j + 1) * P],
                                                   e_normed[:, end * W + j, c * P:(c + 1) * P], ident[:])
                    last.then_inc(turned, 1)

                def mlp_in(b):
                    for m in range(KH):
                        if not (first(b) and m < 2):
                            pe.wait_ge(relu_done, KH * b + m - 1)
                        for k in range(KF):
                            if m == 0:
                                pe.wait_ge(feat_lo_done, KF * b + k + 1)
                            for n, (w, f) in enumerate(((w1_hi, feat_hi), (w1_hi, feat_lo), (w1_lo, feat_hi))):
                                last = nc.tensor.matmul(ps_h[m % 2][:], w[:, k, m * P:(m + 1) * P], f[:, k, :],
                                                        start=(k == 0 and n == 0), stop=(k == KF - 1 and n == 2))
                        last.then_inc(mm1_done, 1)

                def mlp_out(b, g):
                    if g == 0:
                        pe.wait_ge(hid_lo_done, KH * (b + 1))
                    if not first(b):
                        pe.wait_ge(out_lo_done, GROUPS * (b - 1) + g + 1)
                    for a in range(G):
                        at = (G * g + a) * P
                        for m in range(KH):
                            for n, (h, w) in enumerate(((hid_hi, w2_hi), (hid_hi, w2_lo), (hid_lo, w2_hi))):
                                last = nc.tensor.matmul(ps_m[g][:, a * D:(a + 1) * D], h[:, m, at:at + P], w[:, m, :],
                                                        start=(m == 0 and n == 0), stop=(m == KH - 1 and n == 2))
                    last.then_inc(mm2_done, 1)

                def sums(b, q):
                    pe.wait_ge(peers_ready, b + 1)
                    for g in range(GROUPS):
                        pe.wait_ge(out_lo_done, GROUPS * b + g + 1)
                        pe.wait_ge(sums_read, GROUPS * b + g + 1)
                        for a in range(G):
                            for n, part in enumerate((out_hi, out_lo)):
                                for j in range(G * g, G * g + G):
                                    last = nc.tensor.matmul(ps_s[g][:, a * D:(a + 1) * D],
                                                            peers[q][:, j, a * P:(a + 1) * P], part[:, j, :],
                                                            start=(n == 0 and j == G * g),
                                                            stop=(n == 1 and j == G * g + G - 1))
                        last.then_inc(e_summed, 1)

                def step(b, t, q, last=False):
                    mlp_in(b)
                    if not first(b):
                        sums(b - 1, 1 - q)
                    for g in range(GROUPS):
                        if not last:
                            turn(b + 1, 2 * g)
                            turn(b + 1, 2 * g + 1)
                        mlp_out(b, g)

                for k in range(KF):
                    turn(0, k)
                step(0, 0, 0)
                with pe.Fori(0, HALF - 1) as i:
                    step(2 * i + 1, i, 1)
                    step(2 * i + 2, i + 1, 0)
                step(NB - 1, HALF - 1, 1, last=True)
                sums(NB - 1, 1)


_OUT_SPARE = 800


def kernel(**inputs):
    import numpy as _np
    import concourse.bacc as _bacc
    from concourse import mybir as _mybir
    from concourse.bass_utils import run_bass_kernel_spmd as _run

    nc = _bacc.Bacc("TRN2", target_bir_lowering=False, num_devices=1)
    arrays, args = {}, []
    for name in ("x", "src", "dst", "edge_weight", "L1_gnn_W1", "L1_gnn_b1", "L1_gnn_W2", "L1_gnn_b2"):
        a = _np.ascontiguousarray(inputs[name])
        arrays[f"in_{name}"] = a
        args.append(nc.dram_tensor(f"in_{name}", a.shape, _mybir.dt.from_np(a.dtype), kind="ExternalInput").ap())
    nodes, width = inputs["x"].shape
    out = nc.dram_tensor("table_out", (nodes + _OUT_SPARE, width), _mybir.dt.float32, kind="ExternalOutput").ap()
    gnn_preln_two_layers(nc, *args, out)
    r = _run(nc, [arrays], core_ids=[0])
    return r.results[0]["table_out"][:nodes]
```

```python
import concourse.bass as bass
from concourse import mybir
from contextlib import ExitStack


def gnn_preln_two_layers(nc, x, src, dst, edge_weight, w1, b1, w2, b2, out):
    fp32 = mybir.dt.float32
    fp32r = mybir.dt.float32r
    bf16 = mybir.dt.bfloat16
    fp16 = mybir.dt.float16
    i32 = mybir.dt.int32
    ALU = mybir.AluOpType
    ACT = mybir.ActivationFunctionType
    AX = mybir.AxisListType

    P = 128
    N, D = x.shape
    E = src.shape[0]
    HID = w1.shape[1]
    EP = 125
    T = E // EP
    assert EP * T == E
    W = 4
    NB = T // W
    HALF = NB // 2
    G = 2
    ROWS = out.shape[0]
    SPARE = N
    PADKEY = N + W * P
    LO = 128
    C = (PADKEY + P - 1) // LO // P + 1
    KF = 2 * D // P
    KD = D // P
    KH = HID // P
    CW = D + W
    EPS = 1e-5

    BULK = 200
    FLIGHT = 4
    x_flat = x.rearrange("n d -> (n d)").rearrange("(c a w) -> c a w", c=BULK, a=16)
    x1_d = nc.dram_tensor("x1", (ROWS, D), fp32).ap()
    x1_head = x1_d[0:N, :].rearrange("n d -> (n d)").rearrange("(c a w) -> c a w", c=BULK, a=16)
    x1_flat = x1_d.rearrange("n d -> (n d)").rearrange("(c a w) -> c a w", c=BULK, a=16)
    out_flat = out.rearrange("n d -> (n d)").rearrange("(c a w) -> c a w", c=BULK, a=16)
    ZR = ROWS - N
    spare_rows = x1_d[N:ROWS, :].rearrange("(p a) d -> p (a d)", p=100)
    ROUNDS = BULK // FLIGHT
    PREP_ROUNDS = 16
    RING0 = 14
    RING1 = 16
    LAG = 4

    src_rows_d = nc.dram_tensor("src_rows", (T, P), fp32).ap()
    dst_rows_d = nc.dram_tensor("dst_rows", (T, P), fp32).ap()
    hi_rows_d = nc.dram_tensor("hi_rows", (2, T, P), fp16).ap()
    src_rows = src_rows_d.rearrange("(b j) p -> b (j p)", j=W)
    dst_rows = dst_rows_d.rearrange("(b j) p -> b (j p)", j=W)
    hi_rows = hi_rows_d.rearrange("k (b j) p -> b k (j p)", j=W)

    ctx = ExitStack()
    with ctx:
        def sb(name, shape, dt):
            return ctx.enter_context(nc.sbuf_tensor(name, shape, dt))

        def sem(name):
            return ctx.enter_context(nc.semaphore(name))

        keys = sb("keys", [P, 2, T], i32)
        row_idx = sb("row_idx", [P, T], i32)
        weight = sb("weight", [P, T], fp32)
        K_SRC, K_DST, K_SLO, K_DLO, K_VAL = range(5)
        per_edge = sb("per_edge", [P, NB, 5, W], fp32)
        degree = sb("degree", [P, NB, W], fp32)
        eps_col = sb("eps_col", [P, 1], fp32)
        ident = sb("ident", [P, P], fp32)
        hi_ident = sb("hi_ident", [P, C], fp32)
        lo_iota = sb("lo_iota", [P, LO], fp32)
        later = sb("later", [P, P], fp32)
        later_tile = sb("later_tile", [P, W, W], fp32)
        spare = sb("spare", [P, W], fp32)
        table = sb("table", [P, C, 2, LO], bf16)
        b1_col = sb("b1_col", [P, KH], fp32)
        b2_parts = sb("b2_parts", [64, D], fp32r)
        b2_pick = sb("b2_pick", [64, P], fp32r)
        w1_hi = sb("w1_hi", [P, KF, HID], fp32r)
        w1_lo = sb("w1_lo", [P, KF, HID], fp32r)
        w2_hi = sb("w2_hi", [P, KH, D], fp32r)
        w2_lo = sb("w2_lo", [P, KH, D], fp32r)
        waited = sem("waited")

        bulk = [sem(f"bulk{k}") for k in range(FLIGHT)]
        bulk_out = [sem(f"bulk_out{k}") for k in range(FLIGHT)]

        with ExitStack() as stage:
            def sb(name, shape, dt):
                return stage.enter_context(nc.sbuf_tensor(name, shape, dt))

            def pb(name, shape, dt):
                return stage.enter_context(nc.psum_tensor(name, shape, dt))

            keys_f = sb("keys_f", [P, 2, T], fp32)
            hi_i = sb("hi_i", [P, 2, T], i32)
            lo_i = sb("lo_i", [P, 2, T], i32)
            hi_f = sb("hi_f", [P, 2, T], fp32)
            rows_f = sb("rows_f", [P, 2, 2, P], fp32)
            rows_h = sb("rows_h", [P, 2, 2, P], fp16)
            b2_row = sb("b2_row", [64, D], fp32)
            w1_f = sb("w1_f", [P, KF, HID], fp32)
            w2_f = sb("w2_f", [P, KH, D], fp32)
            wd = sb("wd", [P, KD, HID], fp32)
            b1_f = sb("b1_f", [KH, P], fp32)
            zero_rows = sb("zero_rows", [100, ZR * D // 100], fp32)
            zero_bf = sb("zero_bf", [P, 512], bf16)
            hi_iota_i = sb("hi_iota_i", [P, C * P], i32)
            hi_iota = sb("hi_iota", [P, C * P], fp16)
            lo_iota_i = sb("lo_iota_i", [P, LO], i32)
            lo_iota_h = sb("lo_iota_h", [P, LO], fp16)
            hi_ident_i = sb("hi_ident_i", [P, C], i32)
            part_i = sb("part_i", [P, W + 1], i32)
            part_f = sb("part_f", [P, W + 1], fp32)
            hot_hi = sb("hot_hi", [P, W, C * P], bf16)
            hot_lo = sb("hot_lo", [P, W, LO], bf16)
            node_count = sb("node_count", [P, C * P], fp32)
            table_i = sb("table_i", [P, C, LO], i32)
            table_r = sb("table_r", [P, C, LO], i32)
            table_rf = sb("table_rf", [P, C, LO], fp32)
            table_f = sb("table_f", [P, C, LO], fp32)
            CH = C * P // 2
            ps_count = [pb(f"ps_count{h}", [P, 512], fp32) for h in range(2)]
            ps_tab = [pb(f"ps_tab{h}", [P, 512], fp32) for h in range(2)]
            ps_rows = [pb(f"ps_rows{h}", [P, 512], fp32) for h in range(2)]
            ps_b1 = pb("ps_b1", [P, 512], fp32)

            padded = sem("padded")
            consts = sem("consts")
            ident_zero = sem("ident_zero")
            edges_in = sem("edges_in")
            weights_in = sem("weights_in")
            split_keys = sem("split_keys")
            hots_ready = sem("hots_ready")
            hots_free = sem("hots_free")
            counted = sem("counted")
            copied = sem("copied")
            tabled = sem("tabled")
            tab_steps = sem("tab_steps")
            w_steps = sem("w_steps")
            rows_turned = sem("rows_turned")
            rows_copied = sem("rows_copied")
            rows_out = sem("rows_out")
            b1_turned = sem("b1_turned")
            zeroed = sem("zeroed")
            idents_made = sem("idents_made")

            block = stage.enter_context(nc.Block())

            @block.sync
            def _(sp):
                sp.wait_ge(padded, 3)
                sp.dma_start(keys[0:EP, 0, :], src.rearrange("(p t) -> p t", t=T)).then_inc(edges_in, 16)
                sp.dma_start(keys[0:EP, 1, :], dst.rearrange("(p t) -> p t", t=T)).then_inc(edges_in, 16)
                sp.dma_start(weight[0:EP, :], edge_weight.rearrange("(p t) -> p t", t=T)).then_inc(edges_in, 16)
                sp.dma_start(w1_f[:], w1.rearrange("(k p) h -> p k h", p=P)).then_inc(weights_in, 16)
                sp.dma_start(w2_f[:], w2.rearrange("(k p) d -> p k d", p=P)).then_inc(weights_in, 16)
                sp.dma_start(b1_f[:], b1.rearrange("(k p) -> k p", p=P)).then_inc(weights_in, 16)
                sp.dma_start(b2_row[:], b2.partition_broadcast(64)).then_inc(weights_in, 16)
                sp.wait_ge(zeroed, 1)
                sp.dma_start(spare_rows, zero_rows[:]).then_inc(rows_out, 16)
                for k in range(FLIGHT):
                    sp.dma_start(x1_head[k], x_flat[k]).then_inc(bulk[k], 16)
                with sp.Fori(1, PREP_ROUNDS) as r:
                    for k in range(FLIGHT):
                        sp.wait_ge(bulk[k], 16 * r)
                        sp.dma_start(x1_head[bass.ds(FLIGHT * r + k, 1)],
                                     x_flat[bass.ds(FLIGHT * r + k, 1)]).then_inc(bulk[k], 16)
                sp.wait_ge(rows_copied, 2)
                for half, (t0, n) in enumerate(((0, P), (P, T - P))):
                    sp.dma_start(src_rows_d[t0:t0 + n, :], rows_f[0:n, 0, half, :]).then_inc(rows_out, 16)
                    sp.dma_start(dst_rows_d[t0:t0 + n, :], rows_f[0:n, 1, half, :]).then_inc(rows_out, 16)
                    for key in range(2):
                        sp.dma_start(hi_rows_d[key, t0:t0 + n, :],
                                     rows_h[0:n, key, half, :]).then_inc(rows_out, 16)
                sp.wait_ge(rows_out, 16 * 9)

            @block.gpsimd
            def _(pool):
                for key in range(2):
                    nc.gpsimd.iota(keys[:, key, :], [[0, T]], base=PADKEY, channel_multiplier=1).then_inc(padded, 1)
                nc.gpsimd.memset(weight[:], 0.0).then_inc(padded, 1)
                nc.gpsimd.memset(zero_rows[:], 0.0).then_inc(zeroed, 1)
                nc.gpsimd.memset(ident[:], 0.0).then_inc(ident_zero, 1)
                pool.wait_ge(ident_zero, 1)
                nc.gpsimd.affine_select(out=ident[:], in_=ident[:], compare_op=ALU.not_equal, fill=1.0,
                                        base=0, pattern=[[-1, P]], channel_multiplier=1).then_inc(idents_made, 1)
                nc.gpsimd.iota(hi_iota_i[:], [[1, C * P]], base=0, channel_multiplier=0).then_inc(consts, 1)
                nc.gpsimd.iota(lo_iota_i[:], [[1, LO]], base=0, channel_multiplier=0).then_inc(consts, 1)
                nc.gpsimd.iota(hi_ident_i[:], [[P, C]], base=0, channel_multiplier=1).then_inc(consts, 1)
                nc.gpsimd.iota(part_i[:, 0:W], [[P, W]], base=SPARE, channel_multiplier=1).then_inc(consts, 1)
                nc.gpsimd.iota(part_i[:, W:W + 1], [[0, 1]], base=0, channel_multiplier=1).then_inc(consts, 1)

            @block.vector
            def _(dve):
                nc.vector.memset(zero_bf[:], 0.0).then_inc(copied, 1)
                nc.vector.memset(eps_col[:], EPS)
                nc.vector.memset(later_tile[:], 0.0).then_inc(tab_steps, 1)
                dve.wait_ge(tab_steps, 1)
                for a in range(W - 1):
                    nc.vector.memset(later_tile[:, a, a + 1:W], 1.0)
                dve.wait_ge(consts, 5)
                nc.vector.tensor_copy(hi_iota[:], hi_iota_i[:])
                nc.vector.tensor_copy(lo_iota[:], lo_iota_i[:])
                nc.vector.tensor_copy(lo_iota_h[:], lo_iota_i[:])
                nc.vector.tensor_copy(hi_ident[:], hi_ident_i[:])
                nc.vector.tensor_copy(part_f[:], part_i[:]).then_inc(tab_steps, 1)
                dve.wait_ge(tab_steps, 2)
                nc.vector.tensor_copy(spare[:], part_f[:, 0:W])
                nc.vector.tensor_scalar(later[:], lo_iota[:], part_f[:, W:W + 1], None, ALU.is_gt)
                dve.wait_ge(edges_in, 48)
                nc.vector.tensor_scalar(hi_i[:], keys[:], 7, None, ALU.logical_shift_right)
                nc.vector.tensor_scalar(lo_i[:], keys[:], LO - 1, None, ALU.bitwise_and)
                nc.vector.tensor_copy(keys_f[:], keys[:])
                nc.vector.tensor_scalar(row_idx[:], keys[:, 1, :], float(N - 1), None, ALU.min).then_inc(split_keys, 1)
                dve.wait_ge(split_keys, 1)
                nc.vector.tensor_copy(hi_f[:], hi_i[:])
                for kind, what in ((K_SRC, keys_f[:, 0, :]), (K_DST, keys_f[:, 1, :]), (K_SLO, lo_i[:, 0, :]),
                                   (K_DLO, lo_i[:, 1, :]), (K_VAL, weight[:])):
                    nc.vector.tensor_copy(per_edge[:, :, kind, :], what.rearrange("p (b j) -> p b j", j=W))\
                        .then_inc(split_keys, 1)
                dve.wait_ge(split_keys, 6)
                with dve.Fori(0, NB) as b:
                    for j in range(W):
                        dve.wait_ge(hots_free, W * b + j + 1)
                        nc.vector.tensor_scalar(hot_lo[:, j, :], lo_iota_h[:], per_edge[:, bass.ds(b, 1), K_DLO, j:j + 1],
                                                None, ALU.is_equal)
                        nc.vector.tensor_scalar(hot_hi[:, j, :], hi_iota[:], hi_f[:, 1, bass.ds(W * b + j, 1)],
                                                None, ALU.is_equal).then_inc(hots_ready, 1)
                dve.wait_ge(rows_turned, 1)
                for h, n in enumerate((P, T - P)):
                    for key in range(2):
                        at = (2 * h + key) * P
                        nc.vector.tensor_copy(rows_f[0:n, key, h, :], ps_rows[0][0:n, at:at + P])
                        last = nc.vector.tensor_copy(rows_h[0:n, key, h, :], ps_rows[1][0:n, at:at + P])
                last.then_inc(rows_copied, 2)
                dve.wait_ge(b1_turned, 1)
                nc.vector.tensor_copy(b1_col[:], ps_b1[:, 0:KH])
                dve.wait_ge(counted, 1)
                for h in range(2):
                    last = nc.vector.tensor_copy(node_count[:, h * CH:(h + 1) * CH], ps_count[h][:, 0:CH])
                last.then_inc(copied, 1)
                dve.wait_ge(tabled, 1)
                for c in range(C):
                    last = nc.vector.tensor_copy(table_i[:, c, :], ps_tab[c // 4][:, (c % 4) * P:(c % 4 + 1) * P])
                last.then_inc(tab_steps, 1)
                dve.wait_ge(tab_steps, 3)
                nc.vector.tensor_scalar(table_r[:], table_i[:], 255, None, ALU.bitwise_and)
                nc.vector.tensor_copy(table_f[:], table_i[:]).then_inc(tab_steps, 1)
                dve.wait_ge(tab_steps, 4)
                nc.vector.tensor_copy(table_rf[:], table_r[:]).then_inc(tab_steps, 1)
                dve.wait_ge(tab_steps, 5)
                nc.vector.tensor_copy(table[:, :, 1, :], table_rf[:])
                nc.vector.tensor_tensor(table[:, :, 0, :], table_f[:], table_rf[:], ALU.subtract)
                dve.wait_ge(weights_in, 64)
                nc.vector.tensor_tensor(wd[:], w1_f[:, 0:KD, :], w1_f[:, KD:KF, :], ALU.subtract).then_inc(w_steps, 1)
                dve.wait_ge(w_steps, 1)
                nc.vector.tensor_copy(w1_hi[:, 0:KD, :], wd[:])
                nc.vector.tensor_copy(w1_hi[:, KD:KF, :], w1_f[:, KD:KF, :])
                nc.vector.tensor_copy(b2_parts[0:32, :], b2_row[0:32, :])
                nc.vector.tensor_copy(b2_parts[32:64, :], b2_row[32:64, :])
                nc.vector.memset(b2_pick[:].bitcast(fp32), 0.0)
                nc.vector.tensor_copy(w2_hi[:], w2_f[:]).then_inc(w_steps, 1)
                dve.wait_ge(w_steps, 2)
                nc.vector.tensor_tensor(b2_parts[32:64, :], b2_row[32:64, :], b2_parts[32:64, :].bitcast(fp32),
                                        ALU.subtract)
                for row in (0, 32):
                    nc.vector.memset(b2_pick[row:row + 1, :].bitcast(fp32), 1.0)
                nc.vector.tensor_tensor(w1_lo[:, 0:KD, :], wd[:], w1_hi[:, 0:KD, :].bitcast(fp32), ALU.subtract)
                nc.vector.tensor_tensor(w1_lo[:, KD:KF, :], w1_f[:, KD:KF, :],
                                        w1_hi[:, KD:KF, :].bitcast(fp32), ALU.subtract)
                nc.vector.tensor_tensor(w2_lo[:], w2_f[:], w2_hi[:].bitcast(fp32), ALU.subtract)

            @block.tensor
            def _(pe):
                pe.wait_ge(copied, 1)
                for h in range(2):
                    nc.tensor.matmul(ps_count[h][:, 0:CH], zero_bf[:, 0:P], zero_bf[:, 0:CH], start=True, stop=False)
                pe.sem_inc(hots_free, W)
                with pe.Fori(0, NB) as b:
                    for j in range(W):
                        pe.wait_ge(hots_ready, W * b + j + 1)
                        for h in range(2):
                            last = nc.tensor.matmul(ps_count[h][:, 0:CH], hot_lo[:, j, :],
                                                    hot_hi[:, j, h * CH:(h + 1) * CH], start=False, stop=False)
                        last.then_inc(hots_free, 1)
                for h in range(2):
                    last = nc.tensor.matmul(ps_count[h][:, 0:CH], zero_bf[:, 0:P], zero_bf[:, 0:CH],
                                            start=False, stop=True)
                last.then_inc(counted, 1)
                pe.wait_ge(idents_made, 1)
                for w, what in enumerate((keys_f, hi_f)):
                    for half, (t0, n) in enumerate(((0, P), (P, T - P))):
                        for key in range(2):
                            at = (2 * half + key) * P
                            last = nc.tensor.transpose(ps_rows[w][0:n, at:at + P], what[:, key, t0:t0 + n], ident[:])
                last.then_inc(rows_turned, 1)
                pe.wait_ge(weights_in, 64)
                nc.tensor.transpose(ps_b1[:, 0:KH], b1_f[:], ident[0:KH, 0:KH]).then_inc(b1_turned, 1)
                pe.wait_ge(copied, 2)
                for c in range(C):
                    last = nc.tensor.transpose(ps_tab[c // 4][:, (c % 4) * P:(c % 4 + 1) * P],
                                               node_count[:, c * P:(c + 1) * P], ident[:])
                last.then_inc(tabled, 1)

        with ExitStack() as stage:
            def sb(name, shape, dt):
                return stage.enter_context(nc.sbuf_tensor(name, shape, dt))

            def pb(name, shape, dt):
                return stage.enter_context(nc.psum_tensor(name, shape, dt))

            gather_idx = [sb(f"gather_idx{q}", [P, W], i32) for q in range(2)]
            rows = [sb(f"rows{q}", [P, W, D], fp32) for q in range(2)]
            src_row = [sb(f"src_row{q}", [P, W * P], fp32) for q in range(2)]
            hi_row = [sb(f"hi_row{q}", [P, 2, W * P], fp16) for q in range(2)]
            cols = [sb(f"cols{q}", [P, 5, W], fp32) for q in range(2)]
            moments = sb("moments", [P, W, 6], fp32)
            mean_var = [sb(f"mean_var{q}", [P, W, 2], fp32) for q in range(2)]
            std = sb("std", [P, W], fp32)
            rstd = [sb(f"rstd{q}", [P, W], fp32) for q in range(2)]
            shift = [sb(f"shift{q}", [P, W], fp32) for q in range(2)]
            normed = [sb(f"normed{q}", [P, W, D], fp32) for q in range(2)]
            hot = sb("hot", [P, C, 2, W * P], bf16)
            picked = sb("picked", [P, 2, W, LO], bf16)
            deg = [sb(f"deg{q}", [P, 2, W], fp32) for q in range(2)]
            deg_max = sb("deg_max", [P, W], fp32)
            deg_prod = sb("deg_prod", [P, W], fp32)
            root = sb("root", [P, W], fp32)
            inv_root = sb("inv_root", [P, W], fp32)
            coef = [sb(f"coef{q}", [P, W], fp32) for q in range(2)]
            same = sb("same", [P, W, W * P], fp32r)
            same_later = sb("same_later", [P, W, P], bf16)
            dup_in = [sb(f"dup_in{q}", [P, W], fp32) for q in range(2)]
            msg = sb("msg", [P, W, D], fp32)
            msg_hi = sb("msg_hi", [P, W, CW], fp32r)
            msg_lo = sb("msg_lo", [P, W, D], fp32r)
            sums_ring = sb("sums_ring", [P, RING0, W, CW], fp32)
            add_rows = [sb(f"add_rows{q}", [P, W, D], fp32) for q in range(2)]
            dup_tile = sb("dup_tile", [P, W, W], fp32)
            dup = sb("dup", [P, W], fp32)
            dup_all = sb("dup_all", [P, W], fp32)
            is_dup = sb("is_dup", [P, W], fp32)
            to_spare = sb("to_spare", [P, W], fp32)
            move = sb("move", [P, W], fp32)
            scatter_f = sb("scatter_f", [P, W], fp32)
            targets_all = sb("targets_all", [P, NB, W], i32)
            scatter_idx = [sb(f"scatter_idx{q}", [P, W], i32) for q in range(2)]
            ps_deg = [[pb(f"ps_deg{q}{k}", [P, W * P], fp32) for k in range(2)] for q in range(2)]
            ps_sum = [pb(f"ps_sum{a}", [P, 512], fp32) for a in range(W)]

            rows_in = [sem(f"rows_in{q}") for q in range(2)]
            keys_in = [sem(f"keys_in{q}") for q in range(2)]
            add_rows_in = [sem(f"add_rows_in{q}") for q in range(2)]
            keyrows_free = sem("keyrows_free")
            idx_staged = sem("idx_staged")
            moments_done = sem("moments_done")
            var_done = sem("var_done")
            std_done = sem("std_done")
            rstd_done = sem("rstd_done")
            shift_done = sem("shift_done")
            normed_done = sem("normed_done")
            hot_ready = sem("hot_ready")
            deg_ready = sem("deg_ready")
            cols_ready = sem("cols_ready")
            same_ready = sem("same_ready")
            dup_in_done = sem("dup_in_done")
            deg_picked = sem("deg_picked")
            coef_steps = sem("coef_steps")
            root_done = sem("root_done")
            coef_ready = sem("coef_ready")
            msg_ready = sem("msg_ready")
            hi_ready = sem("hi_ready")
            lo_ready = sem("lo_ready")
            summed = sem("summed")
            in_ring = sem("in_ring")
            ring_free = sem("ring_free")
            add_rows_free = sem("add_rows_free")
            idx_steps = sem("idx_steps")
            idx_ready = sem("idx_ready")
            target_staged = sem("target_staged")
            scattered = sem("scattered")
            cnt_cols = sem("cnt_cols")

            block = stage.enter_context(nc.Block())

            @block.sync
            def _(sp):
                with sp.Fori(PREP_ROUNDS, ROUNDS) as r:
                    for k in range(FLIGHT):
                        sp.wait_ge(bulk[k], 16 * r)
                        sp.dma_start(x1_head[bass.ds(FLIGHT * r + k, 1)],
                                     x_flat[bass.ds(FLIGHT * r + k, 1)]).then_inc(bulk[k], 16)
                with sp.Fori(0, HALF) as t:
                    for q in range(2):
                        b = 2 * t + q
                        sp.wait_ge(in_ring, b + 1)
                        sp.wait_ge(add_rows_free, b + 1)
                        sp.sem_inc(waited, 1)
                        sp.dma_start(add_rows[q][:], sums_ring[:, bass.ds(b % RING0, 1), :, 0:D])\
                            .then_inc(add_rows_in[q], 16)

            @block.gpsimd
            def _(pool):
                nc.gpsimd.memset(msg_hi[:, :, D:CW].bitcast(fp32), 0.0).then_inc(cnt_cols, 1)
                pool.wait_ge(cnt_cols, 1)
                for j in range(W):
                    nc.gpsimd.memset(msg_hi[:, j, D + j:D + j + 1].bitcast(fp32), 1.0).then_inc(cnt_cols, 1)
                pool.sem_inc(add_rows_free, 2)
                pool.sem_inc(ring_free, RING0)

                def gather(b, q):
                    pool.wait_ge(normed_done, b + 1)
                    pool.sem_inc(waited, 1)
                    nc.gpsimd.tensor_copy(gather_idx[q][:], row_idx[:, bass.ds(W * b, W)]).then_inc(idx_staged, 1)
                    pool.wait_ge(idx_staged, b + 1)
                    pool.sem_inc(waited, 1)
                    for j in range(W):
                        pool.indirect_dma_start(
                            out=rows[q][:, j, :], out_offset=None, in_=x,
                            in_offset=bass.IndirectOffsetOnAxis(ap=gather_idx[q][:, j:j + 1], axis=0))\
                            .then_inc(rows_in[q], 16)

                def scatter(b, t, q):
                    pool.wait_ge(idx_ready, b + 1)
                    pool.sem_inc(waited, 1)
                    nc.gpsimd.tensor_copy(scatter_idx[q][:], targets_all[:, bass.ds(b, 1), :]).then_inc(target_staged, 1)
                    pool.wait_ge(target_staged, b + 1)
                    pool.wait_ge(add_rows_in[q], 16 * (t + 1))
                    pool.sem_inc(waited, 1)
                    for j in range(W):
                        pool.indirect_dma_start(
                            out=x1_d, out_offset=bass.IndirectOffsetOnAxis(ap=scatter_idx[q][:, j:j + 1], axis=0),
                            in_=add_rows[q][:, j, :], in_offset=None, compute_op=ALU.add)\
                            .then_inc(scattered, 16)

                def scatter_end(b):
                    pool.wait_ge(scattered, 16 * W * (b + 1))
                    pool.sem_inc(add_rows_free, 1)
                    pool.sem_inc(ring_free, 1)

                gather(0, 0)
                gather(1, 1)
                with pool.Fori(1, RING0 // 2) as t:
                    for q in range(2):
                        gather(2 * t + q, q)
                for k in range(FLIGHT):
                    pool.wait_ge(bulk[k], 16 * ROUNDS)
                FAST0 = (RING0 + 2 - LAG - 2) // 2
                with pool.Fori(0, FAST0) as n:
                    for u in range(4):
                        scatter(4 * n + u, 2 * n + u // 2, u % 2)
                        if u % 2 == 0:
                            gather(2 * n + RING0 + u // 2, u // 2)
                        scatter_end(4 * n + u)
                EVEN0 = NB - RING0 - 2 * FAST0
                with pool.Fori(0, EVEN0 // 2) as n:
                    for q in range(2):
                        scatter(2 * n + 4 * FAST0 + q, n + 2 * FAST0, q)
                        gather(2 * n + RING0 + 2 * FAST0 + q, q)
                        scatter_end(2 * n + 4 * FAST0 + q)
                for b in range(4 * FAST0 + EVEN0, NB):
                    scatter(b, b // 2, b % 2)
                    scatter_end(b)

            def following(b, t, q):
                return b + 1, t + q, 1 - q

            @block.vector
            def _(dve):
                dve.sem_inc(keyrows_free, 2)

                def moments_of(b, t, q):
                    dve.wait_ge(rows_in[q], 16 * W * (t + 1))
                    for j in range(W):
                        last = nc.vector.bn_stats(moments[:, j, :], rows[q][:, j, :])
                    last.then_inc(moments_done, 1)
                    dve.wait_ge(moments_done, b + 1)
                    dve.sem_inc(waited, 1)
                    for j in range(W):
                        last = nc.vector.bn_aggr(mean_var[q][:, j, :], moments[:, j, :])
                    last.then_inc(var_done, 1)

                def hots_of(b, t, q):
                    dve.wait_ge(keys_in[q], 32 * (t + 1))
                    dve.wait_ge(deg_ready, b + 1)
                    for c in range(C):
                        last = nc.vector.tensor_scalar(hot[:, c, :, :], hi_row[q][:], hi_ident[:, c:c + 1],
                                                       None, ALU.is_equal)
                    last.then_inc(hot_ready, 1)

                def scales_of(b, t, q):
                    dve.wait_ge(std_done, b + 1)
                    nc.vector.reciprocal(rstd[q][:], std[:]).then_inc(rstd_done, 1)
                    dve.wait_ge(rstd_done, b + 1)
                    nc.vector.scalar_tensor_tensor(shift[q][:], mean_var[q][:, :, 0], -1.0, rstd[q][:],
                                                   ALU.mult, ALU.mult).then_inc(shift_done, 1)

                def degrees_of(b, t, q):
                    dve.wait_ge(cols_ready, b + 1)
                    dve.wait_ge(deg_ready, b + 2)
                    for k, kind in enumerate((K_SLO, K_DLO)):
                        for j in range(W):
                            last = nc.vector.scalar_tensor_tensor(
                                picked[:, k, j, :], lo_iota[:], cols[q][:, kind, j:j + 1],
                                ps_deg[q][k][:, j * P:(j + 1) * P], ALU.is_equal, ALU.mult,
                                accum_out=deg[q][:, k, j:j + 1])
                    last.then_inc(deg_picked, 1)
                    dve.wait_ge(deg_picked, b + 1)
                    nc.vector.tensor_scalar(deg_max[:], deg[q][:, 1, :], 1.0, None, ALU.max).then_inc(coef_steps, 1)
                    dve.wait_ge(coef_steps, 3 * b + 1)
                    nc.vector.scalar_tensor_tensor(deg_prod[:], deg[q][:, 0, :], 1.0, deg_max[:], ALU.max, ALU.mult)\
                        .then_inc(coef_steps, 1)

                def same_of(b, t, q):
                    dve.wait_ge(summed, b + 1)
                    for j in range(W):
                        last = nc.vector.tensor_scalar(same[:, j, :], src_row[q][:], cols[q][:, K_SRC, j:j + 1],
                                                       None, ALU.is_equal)
                    last.then_inc(same_ready, 1)
                    for j in range(W):
                        last = nc.vector.scalar_tensor_tensor(
                            same_later[:, j, :], src_row[q][:, j * P:(j + 1) * P], cols[q][:, K_SRC, j:j + 1],
                            later[:], ALU.is_equal, ALU.mult, accum_out=dup_in[q][:, j:j + 1])
                    last.then_inc(dup_in_done, 1)

                def coef_of(b, t, q):
                    dve.wait_ge(root_done, b + 1)
                    nc.vector.reciprocal(inv_root[:], root[:]).then_inc(coef_steps, 1)
                    dve.wait_ge(coef_steps, 3 * b + 3)
                    nc.vector.tensor_tensor(coef[q][:], inv_root[:], cols[q][:, K_VAL, :], ALU.mult)\
                        .then_inc(coef_ready, 1)
                    dve.wait_ge(dup_in_done, b + 1)
                    dve.sem_inc(keyrows_free, 1)

                def low_of(b, t, q):
                    dve.wait_ge(hi_ready, b + 1)
                    nc.vector.tensor_tensor(msg_lo[:], msg[:], msg_hi[:, :, 0:D].bitcast(fp32), ALU.subtract)\
                        .then_inc(lo_ready, 1)

                def targets_of(b, t, q):
                    dve.wait_ge(in_ring, b + 1)
                    nc.vector.tensor_tensor(dup_tile[:], sums_ring[:, bass.ds(b % RING0, 1), :, D:CW]
                                            .rearrange("p o j c -> p (o j) c"), later_tile[:], ALU.mult)\
                        .then_inc(idx_steps, 1)
                    nc.vector.tensor_tensor(to_spare[:], spare[:], cols[q][:, K_SRC, :], ALU.subtract)
                    dve.wait_ge(idx_steps, 6 * b + 1)
                    nc.vector.tensor_reduce(dup[:], dup_tile[:], AX.X, ALU.add).then_inc(idx_steps, 1)
                    dve.wait_ge(idx_steps, 6 * b + 2)
                    nc.vector.tensor_tensor(dup_all[:], dup[:], dup_in[q][:], ALU.add).then_inc(idx_steps, 1)
                    dve.wait_ge(idx_steps, 6 * b + 3)
                    nc.vector.tensor_scalar(is_dup[:], dup_all[:], 0.5, None, ALU.is_gt).then_inc(idx_steps, 1)
                    dve.wait_ge(idx_steps, 6 * b + 4)
                    nc.vector.tensor_tensor(move[:], is_dup[:], to_spare[:], ALU.mult).then_inc(idx_steps, 1)
                    dve.wait_ge(idx_steps, 6 * b + 5)
                    nc.vector.tensor_tensor(scatter_f[:], move[:], cols[q][:, K_SRC, :], ALU.add).then_inc(idx_steps, 1)
                    dve.wait_ge(idx_steps, 6 * b + 6)
                    dve.sem_inc(waited, 1)
                    nc.vector.tensor_copy(targets_all[:, bass.ds(b, 1), :], scatter_f[:]).then_inc(idx_ready, 1)

                def columns_of(b, t, q):
                    nc.vector.tensor_copy(cols[q][:], per_edge[:, bass.ds(b, 1), :, :]).then_inc(cols_ready, 1)

                def keep_degree(b, t, q):
                    nc.vector.tensor_copy(degree[:, bass.ds(b, 1), :], deg[q][:, 1, :])

                def step(b, t, q, first=False, last=False):
                    nxt = following(b, t, q)
                    if not last:
                        hots_of(*nxt)
                    degrees_of(b, t, q)
                    same_of(b, t, q)
                    coef_of(b, t, q)
                    keep_degree(b, t, q)
                    if not last:
                        moments_of(*nxt)
                    if not first:
                        targets_of(b - 1, t - 1 + q, 1 - q)
                    if not last:
                        columns_of(*nxt)
                        scales_of(*nxt)
                    low_of(b, t, q)

                hots_of(0, 0, 0)
                moments_of(0, 0, 0)
                columns_of(0, 0, 0)
                scales_of(0, 0, 0)
                step(0, 0, 0, first=True)
                with dve.Fori(0, HALF - 1) as i:
                    step(2 * i + 1, i, 1)
                    step(2 * i + 2, i + 1, 0)
                step(NB - 1, HALF - 1, 1, last=True)
                targets_of(NB - 1, HALF - 1, 1)

            @block.scalar
            def _(act):
                act.sem_inc(normed_done, 2)

                def load_keys(b, q):
                    act.wait_ge(keyrows_free, b + 1)
                    act.dma_start(src_row[q][:], src_rows[bass.ds(b, 1), :].partition_broadcast(P))\
                        .then_inc(keys_in[q], 16)
                    act.dma_start(hi_row[q][:], hi_rows[bass.ds(b, 1), :, :].partition_broadcast(P))\
                        .then_inc(keys_in[q], 16)

                def std_of(b, t, q):
                    act.wait_ge(var_done, b + 1)
                    if not (isinstance(b, int) and b == 0):
                        act.wait_ge(rstd_done, b)
                    nc.scalar.activation(std[:], mean_var[q][:, :, 1], ACT.Sqrt, bias=eps_col[:]).then_inc(std_done, 1)

                def norm(b, t, q):
                    act.wait_ge(shift_done, b + 1)
                    for j in range(W):
                        last = nc.scalar.activation(normed[q][:, j, :], rows[q][:, j, :], ACT.Relu,
                                                    bias=shift[q][:, j:j + 1], scale=rstd[q][:, j:j + 1])
                    last.then_inc(normed_done, 1)

                def root_of(b, t, q):
                    act.wait_ge(coef_steps, 3 * b + 2)
                    nc.scalar.activation(root[:], deg_prod[:], ACT.Sqrt).then_inc(root_done, 1)

                def message(b, t, q):
                    act.wait_ge(normed_done, b + 3)
                    act.wait_ge(coef_ready, b + 1)
                    act.wait_ge(summed, b + 1)
                    for j in range(W):
                        last = nc.scalar.activation(msg[:, j, :], normed[q][:, j, :], ACT.Copy,
                                                    scale=coef[q][:, j:j + 1])
                    last.then_inc(msg_ready, 1)
                    act.wait_ge(msg_ready, b + 1)
                    nc.scalar.activation(msg_hi[:, :, 0:D], msg[:], ACT.Copy).then_inc(hi_ready, 1)

                def to_ring(b, t, q):
                    act.wait_ge(summed, b + 2)
                    act.wait_ge(ring_free, b + 1)
                    act.sem_inc(waited, 1)
                    for j in range(W):
                        last = nc.scalar.activation(sums_ring[:, bass.ds(b % RING0, 1), j, :], ps_sum[j][:, 0:CW],
                                                    ACT.Copy)
                    last.then_inc(in_ring, 1)

                def step(b, t, q, first=False, last=False, load=True):
                    root_of(b, t, q)
                    if not first:
                        to_ring(b - 1, t - 1 + q, 1 - q)
                    message(b, t, q)
                    if load:
                        load_keys(b + 2, q)
                    if not last:
                        std_of(*following(b, t, q))
                        norm(*following(b, t, q))

                load_keys(0, 0)
                load_keys(1, 1)
                std_of(0, 0, 0)
                norm(0, 0, 0)
                step(0, 0, 0, first=True)
                with act.Fori(0, HALF - 2) as i:
                    step(2 * i + 1, i, 1)
                    step(2 * i + 2, i + 1, 0)
                step(NB - 3, HALF - 2, 1)
                step(NB - 2, HALF - 1, 0, load=False)
                step(NB - 1, HALF - 1, 1, last=True, load=False)
                to_ring(NB - 1, HALF - 1, 1)

            @block.tensor
            def _(pe):
                pe.sem_inc(deg_ready, 1)
                pe.sem_inc(summed, 1)
                pe.wait_ge(cnt_cols, 1 + W)

                def degrees(b, q):
                    pe.wait_ge(hot_ready, b + 1)
                    if not (isinstance(b, int) and b < 2):
                        pe.wait_ge(deg_picked, b - 1)
                    for k in range(2):
                        for j in range(W):
                            for c in range(C):
                                for part in range(2):
                                    last = nc.tensor.matmul(ps_deg[q][k][:, j * P:(j + 1) * P],
                                                            hot[:, c, k, j * P:(j + 1) * P], table[:, c, part, :],
                                                            start=(c == 0 and part == 0),
                                                            stop=(c == C - 1 and part == 1))
                    last.then_inc(deg_ready, 1)

                def sums(b):
                    pe.wait_ge(same_ready, b + 1)
                    pe.wait_ge(lo_ready, b + 1)
                    if not (isinstance(b, int) and b == 0):
                        pe.wait_ge(in_ring, b)
                    for a in range(W):
                        for j in range(W):
                            nc.tensor.matmul(ps_sum[a][:, 0:CW], same[:, j, a * P:(a + 1) * P], msg_hi[:, j, :],
                                             start=(j == 0), stop=False)
                        for j in range(W):
                            last = nc.tensor.matmul(ps_sum[a][:, 0:D], same[:, j, a * P:(a + 1) * P], msg_lo[:, j, :],
                                                    start=False, stop=(j == W - 1))
                    last.then_inc(summed, 1)

                degrees(0, 0)
                degrees(1, 1)
                sums(0)
                with pe.Fori(0, HALF - 1) as i:
                    degrees(2 * i + 2, 0)
                    sums(2 * i + 1)
                    degrees(2 * i + 3, 1)
                    sums(2 * i + 2)
                sums(NB - 1)

        with ExitStack() as stage:
            def sb(name, shape, dt):
                return stage.enter_context(nc.sbuf_tensor(name, shape, dt))

            def pb(name, shape, dt):
                return stage.enter_context(nc.psum_tensor(name, shape, dt))

            ends_idx = [sb(f"ends_idx{q}", [P, 2, W], i32) for q in range(2)]
            ends = [sb(f"ends{q}", [P, 2 * W, D], fp32) for q in range(2)]
            dst_row = [sb(f"dst_row{q}", [P, W * P], fp32) for q in range(2)]
            e_moments = sb("e_moments", [P, 2 * W, 6], fp32)
            e_mean_var = [sb(f"e_mean_var{q}", [P, 2 * W, 2], fp32) for q in range(2)]
            e_std = sb("e_std", [P, 2 * W], fp32)
            e_rstd = [sb(f"e_rstd{q}", [P, 2 * W], fp32) for q in range(2)]
            e_shift = [sb(f"e_shift{q}", [P, 2 * W], fp32) for q in range(2)]
            e_normed = sb("e_normed", [P, 2 * W, D], fp32)
            feat_hi = sb("feat_hi", [P, KF, W * P], fp32r)
            feat_lo = sb("feat_lo", [P, KF, W * P], fp32r)
            hid = [sb(f"hid{h}", [P, W * P], fp32) for h in range(2)]
            hid_hi = sb("hid_hi", [P, KH, W * P], fp32r)
            hid_lo = sb("hid_lo", [P, KH, W * P], fp32r)
            out_hi = sb("out_hi", [P, W, D], fp32r)
            out_lo = sb("out_lo", [P, W, D], fp32r)
            dst_col = [sb(f"dst_col{q}", [P, W], fp32) for q in range(2)]
            deg_col = [sb(f"deg_col{q}", [P, W], fp32) for q in range(2)]
            deg_eps = sb("deg_eps", [P, W], fp32)
            inv_deg = [sb(f"inv_deg{q}", [P, W], fp32) for q in range(2)]
            peers = [sb(f"peers{q}", [P, W, G * P], fp32r) for q in range(2)]
            after = sb("after", [P, G, G * P], fp32)
            peers_after = sb("peers_after", [P, W, G * P], bf16)
            n_after = sb("n_after", [P, W], fp32)
            e_is_dup = sb("e_is_dup", [P, W], fp32)
            e_to_spare = sb("e_to_spare", [P, W], fp32)
            e_move = sb("e_move", [P, W], fp32)
            e_target = sb("e_target", [P, W], fp32)
            e_targets_all = sb("e_targets_all", [P, NB, W], i32)
            target_idx = [sb(f"target_idx{q}", [P, W], i32) for q in range(2)]
            e_ring = sb("e_ring", [P, RING1, W, D], fp32)
            e_add_rows = [sb(f"e_add_rows{q}", [P, W, D], fp32) for q in range(2)]
            ps_t = [pb(f"ps_t{h}", [P, W * P], fp32) for h in range(2)]
            ps_h = [pb(f"ps_h{h}", [P, W * P], fp32) for h in range(2)]
            ps_m = [pb(f"ps_m{h}", [P, G * D], fp32) for h in range(2)]
            ps_s = [pb(f"ps_s{h}", [P, G * D], fp32) for h in range(2)]

            ends_in = [sem(f"ends_in{q}") for q in range(2)]
            dst_row_in = [sem(f"dst_row_in{q}") for q in range(2)]
            dst_row_free = sem("dst_row_free")
            ends_staged = sem("ends_staged")
            e_moments_done = sem("e_moments_done")
            e_var_done = sem("e_var_done")
            e_std_done = sem("e_std_done")
            e_rstd_done = sem("e_rstd_done")
            e_shift_done = sem("e_shift_done")
            e_normed_done = sem("e_normed_done")
            turned = sem("turned")
            feat_hi_done = sem("feat_hi_done")
            feat_lo_done = sem("feat_lo_done")
            mm1_done = sem("mm1_done")
            relu_done = sem("relu_done")
            hid_hi_done = sem("hid_hi_done")
            hid_lo_done = sem("hid_lo_done")
            mm2_done = sem("mm2_done")
            out_hi_done = sem("out_hi_done")
            out_lo_done = sem("out_lo_done")
            e_cols_done = sem("e_cols_done")
            e_deg_done = sem("e_deg_done")
            inv_deg_done = sem("inv_deg_done")
            after_made = sem("after_made")
            peers_ready = sem("peers_ready")
            n_after_done = sem("n_after_done")
            e_idx_steps = sem("e_idx_steps")
            e_target_staged = sem("e_target_staged")
            e_target_ready = sem("e_target_ready")
            e_summed = sem("e_summed")
            e_in_ring = sem("e_in_ring")
            e_ring_free = sem("e_ring_free")
            e_add_in = [sem(f"e_add_in{q}") for q in range(2)]
            e_add_free = sem("e_add_free")
            e_scattered = sem("e_scattered")

            GROUPS = W // G
            block = stage.enter_context(nc.Block())

            def following(b, t, q):
                return b + 1, t + q, 1 - q

            def first(b):
                return isinstance(b, int) and b == 0

            @block.sync
            def _(sp):
                for k in range(FLIGHT):
                    sp.dma_start(out_flat[k], x1_flat[k]).then_inc(bulk_out[k], 16)
                with sp.Fori(1, ROUNDS) as r:
                    for k in range(FLIGHT):
                        sp.wait_ge(bulk_out[k], 16 * r)
                        sp.dma_start(out_flat[bass.ds(FLIGHT * r + k, 1)],
                                     x1_flat[bass.ds(FLIGHT * r + k, 1)]).then_inc(bulk_out[k], 16)
                with sp.Fori(0, HALF) as t:
                    for q in range(2):
                        b = 2 * t + q
                        sp.wait_ge(e_in_ring, GROUPS * (b + 2))
                        sp.sem_inc(waited, 1)
                        sp.wait_ge(e_add_free, b + 1)
                        sp.sem_inc(waited, 1)
                        sp.dma_start(e_add_rows[q][:], e_ring[:, bass.ds(b % RING1, 1), :, :])\
                            .then_inc(e_add_in[q], 16)

            @block.gpsimd
            def _(pool):
                pool.sem_inc(e_add_free, 2)
                pool.sem_inc(e_ring_free, RING1)

                def gather(b, q, end):
                    if end == 0:
                        pool.wait_ge(e_normed_done, b + 1)
                        pool.sem_inc(waited, 1)
                        nc.gpsimd.tensor_copy(ends_idx[q][:], keys[:, :, bass.ds(W * b, W)]).then_inc(ends_staged, 1)
                        pool.wait_ge(ends_staged, b + 1)
                        pool.sem_inc(waited, 1)
                    for j in range(W):
                        pool.indirect_dma_start(
                            out=ends[q][:, end * W + j, :], out_offset=None, in_=x1_d,
                            in_offset=bass.IndirectOffsetOnAxis(ap=ends_idx[q][:, 1 - end, j:j + 1], axis=0))\
                            .then_inc(ends_in[q], 16)

                def scatter(b, t, q, g):
                    if g == 0:
                        pool.wait_ge(e_target_ready, b + 1)
                        pool.sem_inc(waited, 1)
                        nc.gpsimd.tensor_copy(target_idx[q][:], e_targets_all[:, bass.ds(b, 1), :])\
                            .then_inc(e_target_staged, 1)
                        pool.wait_ge(e_target_staged, b + 1)
                        pool.wait_ge(e_add_in[q], 16 * (t + 1))
                        pool.sem_inc(waited, 1)
                    for j in range(G * g, G * g + G):
                        pool.indirect_dma_start(
                            out=out, out_offset=bass.IndirectOffsetOnAxis(ap=target_idx[q][:, j:j + 1], axis=0),
                            in_=e_add_rows[q][:, j, :], in_offset=None, compute_op=ALU.add)\
                            .then_inc(e_scattered, 16)

                def scatter_end(b, g):
                    pool.wait_ge(e_scattered, 16 * G * (GROUPS * b + g + 1))
                    pool.sem_inc(waited, 1)
                    if g == GROUPS - 1:
                        pool.sem_inc(e_add_free, 1)
                        pool.sem_inc(e_ring_free, 1)

                for b in range(2):
                    gather(b, b, 0)
                    gather(b, b, 1)
                with pool.Fori(1, RING1 // 2) as t:
                    for q in range(2):
                        gather(2 * t + q, q, 0)
                        gather(2 * t + q, q, 1)
                for k in range(FLIGHT):
                    pool.wait_ge(bulk_out[k], 16 * ROUNDS)
                FAST1 = (RING1 - LAG) // 2
                with pool.Fori(0, FAST1) as n:
                    for u in range(6):
                        for g in range(GROUPS):
                            scatter(6 * n + u, 3 * n + u // 2, u % 2, g)
                            slot = GROUPS * u + g
                            if slot % 3 != 2:
                                half = slot // 3 * 2 + slot % 3
                                gather(4 * n + RING1 + half // 2, half // 2 % 2, half % 2)
                            scatter_end(6 * n + u, g)
                EVEN1 = NB - RING1 - 4 * FAST1
                with pool.Fori(0, EVEN1 // 2) as n:
                    for q in range(2):
                        for g in range(GROUPS):
                            scatter(2 * n + 6 * FAST1 + q, n + 3 * FAST1, q, g)
                            gather(2 * n + RING1 + 4 * FAST1 + q, q, g)
                            scatter_end(2 * n + 6 * FAST1 + q, g)
                for b in range(6 * FAST1 + EVEN1, NB):
                    for g in range(GROUPS):
                        scatter(b, b // 2, b % 2, g)
                        scatter_end(b, g)

            @block.vector
            def _(dve):
                dve.sem_inc(dst_row_free, 2)
                nc.vector.memset(after[:], 0.0).then_inc(after_made, 1)
                dve.wait_ge(after_made, 1)
                nc.vector.memset(after[:, 0, P:G * P], 1.0)
                nc.vector.tensor_copy(after[:, 0, 0:P], later[:])
                nc.vector.tensor_copy(after[:, 1, P:G * P], later[:]).then_inc(after_made, 1)
                dve.wait_ge(after_made, 2)

                def moments_of(b, t, q):
                    dve.wait_ge(ends_in[q], 16 * 2 * W * (t + 1))
                    for r in range(2 * W):
                        last = nc.vector.bn_stats(e_moments[:, r, :], ends[q][:, r, :])
                    last.then_inc(e_moments_done, 1)
                    dve.wait_ge(e_moments_done, b + 1)
                    dve.sem_inc(waited, 1)
                    for r in range(2 * W):
                        last = nc.vector.bn_aggr(e_mean_var[q][:, r, :], e_moments[:, r, :])
                    last.then_inc(e_var_done, 1)

                def scales_of(b, t, q):
                    dve.wait_ge(e_std_done, b + 1)
                    nc.vector.reciprocal(e_rstd[q][:], e_std[:]).then_inc(e_rstd_done, 1)
                    dve.wait_ge(e_rstd_done, b + 1)
                    nc.vector.scalar_tensor_tensor(e_shift[q][:], e_mean_var[q][:, :, 0], -1.0, e_rstd[q][:],
                                                   ALU.mult, ALU.mult).then_inc(e_shift_done, 1)

                def peers_of(b, t, q):
                    nc.vector.tensor_copy(dst_col[q][:], per_edge[:, bass.ds(b, 1), K_DST, :])
                    nc.vector.tensor_copy(deg_col[q][:], degree[:, bass.ds(b, 1), :]).then_inc(e_cols_done, 1)
                    dve.wait_ge(e_cols_done, b + 1)
                    nc.vector.tensor_scalar(deg_eps[:], deg_col[q][:], 1e-8, None, ALU.add).then_inc(e_deg_done, 1)
                    dve.wait_ge(dst_row_in[q], 16 * (t + 1))
                    dve.wait_ge(e_summed, GROUPS * b)
                    for j in range(W):
                        g = j // G
                        last = nc.vector.tensor_scalar(peers[q][:, j, :], dst_row[q][:, g * G * P:(g + 1) * G * P],
                                                       dst_col[q][:, j:j + 1], None, ALU.is_equal)
                    last.then_inc(peers_ready, 1)

                def after_of(b, t, q):
                    for j in range(W):
                        g = j // G
                        last = nc.vector.scalar_tensor_tensor(
                            peers_after[:, j, :], dst_row[q][:, g * G * P:(g + 1) * G * P], dst_col[q][:, j:j + 1],
                            after[:, j % G, :], ALU.is_equal, ALU.mult, accum_out=n_after[:, j:j + 1])
                    last.then_inc(n_after_done, 1)
                    dve.wait_ge(e_deg_done, b + 1)
                    dve.wait_ge(e_in_ring, GROUPS * b)
                    nc.vector.reciprocal(inv_deg[q][:], deg_eps[:]).then_inc(inv_deg_done, 1)
                    nc.vector.tensor_tensor(e_to_spare[:], spare[:], dst_col[q][:], ALU.subtract)

                def targets_of(b, t, q):
                    dve.wait_ge(n_after_done, b + 1)
                    dve.sem_inc(dst_row_free, 1)
                    nc.vector.tensor_scalar(e_is_dup[:], n_after[:], 0.5, None, ALU.is_gt).then_inc(e_idx_steps, 1)
                    dve.wait_ge(e_idx_steps, 3 * b + 1)
                    nc.vector.tensor_tensor(e_move[:], e_is_dup[:], e_to_spare[:], ALU.mult).then_inc(e_idx_steps, 1)
                    dve.wait_ge(e_idx_steps, 3 * b + 2)
                    nc.vector.tensor_tensor(e_target[:], e_move[:], dst_col[q][:], ALU.add).then_inc(e_idx_steps, 1)
                    dve.wait_ge(e_idx_steps, 3 * b + 3)
                    dve.sem_inc(waited, 1)
                    nc.vector.tensor_copy(e_targets_all[:, bass.ds(b, 1), :], e_target[:]).then_inc(e_target_ready, 1)

                def hid_low(b, m):
                    dve.wait_ge(hid_hi_done, KH * b + m + 1)
                    nc.vector.tensor_tensor(hid_lo[:, m, :], hid[m % 2][:], hid_hi[:, m, :].bitcast(fp32),
                                            ALU.subtract).then_inc(hid_lo_done, 1)

                def feat_low(b, k):
                    dve.wait_ge(feat_hi_done, KF * b + k + 1)
                    nc.vector.tensor_tensor(feat_lo[:, k, :], ps_t[k % 2][:], feat_hi[:, k, :].bitcast(fp32),
                                            ALU.subtract).then_inc(feat_lo_done, 1)

                def out_low(b, g):
                    dve.wait_ge(out_hi_done, GROUPS * b + g + 1)
                    nc.vector.tensor_tensor(out_lo[:, G * g:G * g + G, :].rearrange("p a d -> p (a d)"), ps_m[g][:],
                                            out_hi[:, G * g:G * g + G, :].rearrange("p a d -> p (a d)").bitcast(fp32),
                                            ALU.subtract).then_inc(out_lo_done, 1)

                def step(b, t, q, last=False):
                    if not last:
                        moments_of(*following(b, t, q))
                    hid_low(b, 0)
                    if not last:
                        scales_of(*following(b, t, q))
                    peers_of(b, t, q)
                    hid_low(b, 1)
                    after_of(b, t, q)
                    hid_low(b, 2)
                    targets_of(b, t, q)
                    hid_low(b, 3)
                    for g in range(GROUPS):
                        if not last:
                            feat_low(b + 1, 2 * g)
                            feat_low(b + 1, 2 * g + 1)
                        out_low(b, g)

                moments_of(0, 0, 0)
                scales_of(0, 0, 0)
                for k in range(KF):
                    feat_low(0, k)
                step(0, 0, 0)
                with dve.Fori(0, HALF - 1) as i:
                    step(2 * i + 1, i, 1)
                    step(2 * i + 2, i + 1, 0)
                step(NB - 1, HALF - 1, 1, last=True)

            @block.scalar
            def _(act):
                act.sem_inc(e_normed_done, 2)
                act.sem_inc(e_in_ring, GROUPS)

                def load_keys(b, q):
                    act.wait_ge(dst_row_free, b + 1)
                    act.dma_start(dst_row[q][:], dst_rows[bass.ds(b, 1), :].partition_broadcast(P))\
                        .then_inc(dst_row_in[q], 16)

                def std_of(b, t, q):
                    act.wait_ge(e_var_done, b + 1)
                    if not first(b):
                        act.wait_ge(e_rstd_done, b)
                    nc.scalar.activation(e_std[:], e_mean_var[q][:, :, 1], ACT.Sqrt, bias=eps_col[:])\
                        .then_inc(e_std_done, 1)

                def norm(b, t, q, r0, r1):
                    if r0 == 0:
                        act.wait_ge(e_shift_done, b + 1)
                        if not first(b):
                            act.wait_ge(turned, KF * b)
                    for r in range(r0, r1):
                        last = nc.scalar.activation(e_normed[:, r, :], ends[q][:, r, :], ACT.Relu,
                                                    bias=e_shift[q][:, r:r + 1], scale=e_rstd[q][:, r:r + 1])
                    if r1 == 2 * W:
                        last.then_inc(e_normed_done, 1)

                def feat_high(b, k):
                    act.wait_ge(turned, KF * b + k + 1)
                    nc.scalar.activation(feat_hi[:, k, :], ps_t[k % 2][:], ACT.Copy).then_inc(feat_hi_done, 1)

                def hid_high(b, m):
                    act.wait_ge(mm1_done, KH * b + m + 1)
                    if not (first(b) and m < 2):
                        act.wait_ge(hid_lo_done, KH * b + m - 1)
                    nc.scalar.activation(hid[m % 2][:], ps_h[m % 2][:], ACT.Relu, bias=b1_col[:, m:m + 1])\
                        .then_inc(relu_done, 1)
                    act.wait_ge(relu_done, KH * b + m + 1)
                    nc.scalar.activation(hid_hi[:, m, :], hid[m % 2][:], ACT.Copy).then_inc(hid_hi_done, 1)

                def out_high(b, g):
                    act.wait_ge(mm2_done, GROUPS * b + g + 1)
                    nc.scalar.activation(out_hi[:, G * g:G * g + G, :].rearrange("p a d -> p (a d)"), ps_m[g][:],
                                         ACT.Copy).then_inc(out_hi_done, 1)

                def scale(b, q, g):
                    act.wait_ge(e_summed, GROUPS * (b + 1) + g + 1)
                    act.wait_ge(e_ring_free, b + 1)
                    act.wait_ge(inv_deg_done, b + 1)
                    act.sem_inc(waited, 1)
                    for a in range(G):
                        j = G * g + a
                        last = nc.scalar.activation(e_ring[:, bass.ds(b % RING1, 1), j, :], ps_s[g][:, a * D:(a + 1) * D],
                                                    ACT.Copy, scale=inv_deg[q][:, j:j + 1])
                    last.then_inc(e_in_ring, 1)

                def step(b, t, q, last=False, load=True):
                    nxt = following(b, t, q)
                    hid_high(b, 0)
                    if not last:
                        std_of(*nxt)
                        norm(*nxt, 0, 2)
                    hid_high(b, 1)
                    if not last:
                        norm(*nxt, 2, 5)
                    hid_high(b, 2)
                    if not last:
                        norm(*nxt, 5, 8)
                    hid_high(b, 3)
                    for g in range(GROUPS):
                        if not last:
                            feat_high(b + 1, 2 * g)
                            feat_high(b + 1, 2 * g + 1)
                        if not first(b):
                            scale(b - 1, 1 - q, g)
                        out_high(b, g)
                    if load:
                        load_keys(b + 2, q)

                load_keys(0, 0)
                load_keys(1, 1)
                std_of(0, 0, 0)
                norm(0, 0, 0, 0, 2 * W)
                for k in range(KF):
                    feat_high(0, k)
                step(0, 0, 0)
                with act.Fori(0, HALF - 2) as i:
                    step(2 * i + 1, i, 1)
                    step(2 * i + 2, i + 1, 0)
                step(NB - 3, HALF - 2, 1)
                step(NB - 2, HALF - 1, 0, load=False)
                step(NB - 1, HALF - 1, 1, last=True, load=False)
                for g in range(GROUPS):
                    scale(NB - 1, 1, g)

            @block.tensor
            def _(pe):
                pe.sem_inc(e_summed, GROUPS)

                def turn(b, k):
                    if k == 0:
                        pe.wait_ge(e_normed_done, b + 3)
                    if not (first(b) and k < 2):
                        pe.wait_ge(feat_lo_done, KF * b + k - 1)
                    end, c = k // KD, k % KD
                    for j in range(W):
                        last = nc.tensor.transpose(ps_t[k % 2][:, j * P:(j + 1) * P],
                                                   e_normed[:, end * W + j, c * P:(c + 1) * P], ident[:])
                    last.then_inc(turned, 1)

                def mlp_in(b):
                    for m in range(KH):
                        if not (first(b) and m < 2):
                            pe.wait_ge(relu_done, KH * b + m - 1)
                        for k in range(KF):
                            if m == 0:
                                pe.wait_ge(feat_lo_done, KF * b + k + 1)
                            for n, (w, f) in enumerate(((w1_hi, feat_hi), (w1_hi, feat_lo), (w1_lo, feat_hi))):
                                last = nc.tensor.matmul(ps_h[m % 2][:], w[:, k, m * P:(m + 1) * P], f[:, k, :],
                                                        start=(k == 0 and n == 0), stop=(k == KF - 1 and n == 2))
                        last.then_inc(mm1_done, 1)

                def mlp_out(b, g):
                    if g == 0:
                        pe.wait_ge(hid_lo_done, KH * (b + 1))
                    if not first(b):
                        pe.wait_ge(out_lo_done, GROUPS * (b - 1) + g + 1)
                    for a in range(G):
                        at = (G * g + a) * P
                        for m in range(KH):
                            for n, (h, w) in enumerate(((hid_hi, w2_hi), (hid_hi, w2_lo), (hid_lo, w2_hi))):
                                nc.tensor.matmul(ps_m[g][:, a * D:(a + 1) * D], h[:, m, at:at + P], w[:, m, :],
                                                 start=(m == 0 and n == 0), stop=False)
                        last = nc.tensor.matmul(ps_m[g][:, a * D:(a + 1) * D], b2_pick[:], b2_parts[:],
                                                start=False, stop=True)
                    last.then_inc(mm2_done, 1)

                def sums(b, q):
                    pe.wait_ge(peers_ready, b + 1)
                    for g in range(GROUPS):
                        pe.wait_ge(out_lo_done, GROUPS * b + g + 1)
                        pe.wait_ge(e_in_ring, GROUPS * b + g + 1)
                        for a in range(G):
                            for n, part in enumerate((out_hi, out_lo)):
                                for j in range(G * g, G * g + G):
                                    last = nc.tensor.matmul(ps_s[g][:, a * D:(a + 1) * D],
                                                            peers[q][:, j, a * P:(a + 1) * P], part[:, j, :],
                                                            start=(n == 0 and j == G * g),
                                                            stop=(n == 1 and j == G * g + G - 1))
                        last.then_inc(e_summed, 1)

                def step(b, t, q, last=False):
                    mlp_in(b)
                    if not first(b):
                        sums(b - 1, 1 - q)
                    for g in range(GROUPS):
                        if not last:
                            turn(b + 1, 2 * g)
                            turn(b + 1, 2 * g + 1)
                        mlp_out(b, g)

                for k in range(KF):
                    turn(0, k)
                step(0, 0, 0)
                with pe.Fori(0, HALF - 1) as i:
                    step(2 * i + 1, i, 1)
                    step(2 * i + 2, i + 1, 0)
                step(NB - 1, HALF - 1, 1, last=True)
                sums(NB - 1, 1)


_OUT_SPARE = 800


def kernel(**inputs):
    import numpy as _np
    import concourse.bacc as _bacc
    from concourse import mybir as _mybir
    from concourse.bass_utils import run_bass_kernel_spmd as _run

    nc = _bacc.Bacc("TRN2", target_bir_lowering=False, num_devices=1)
    arrays, args = {}, []
    for name in ("x", "src", "dst", "edge_weight", "L1_gnn_W1", "L1_gnn_b1", "L1_gnn_W2", "L1_gnn_b2"):
        a = _np.ascontiguousarray(inputs[name])
        arrays[f"in_{name}"] = a
        args.append(nc.dram_tensor(f"in_{name}", a.shape, _mybir.dt.from_np(a.dtype), kind="ExternalInput").ap())
    nodes, width = inputs["x"].shape
    out = nc.dram_tensor("table_out", (nodes + _OUT_SPARE, width), _mybir.dt.float32, kind="ExternalOutput").ap()
    gnn_preln_two_layers(nc, *args, out)
    r = _run(nc, [arrays], core_ids=[0])
    return r.results[0]["table_out"][:nodes]
```

```python
import concourse.bass as bass
from concourse import mybir
from contextlib import ExitStack


def gnn_preln_two_layers(nc, x, src, dst, edge_weight, w1, b1, w2, b2, out):
    fp32 = mybir.dt.float32
    fp32r = mybir.dt.float32r
    bf16 = mybir.dt.bfloat16
    fp16 = mybir.dt.float16
    i32 = mybir.dt.int32
    ALU = mybir.AluOpType
    ACT = mybir.ActivationFunctionType
    AX = mybir.AxisListType

    P = 128
    N, D = x.shape
    E = src.shape[0]
    HID = w1.shape[1]
    EP = 125
    T = E // EP
    assert EP * T == E
    W = 4
    NB = T // W
    HALF = NB // 2
    G = 2
    ROWS = out.shape[0]
    SPARE = N
    PADKEY = N + W * P
    LO = 128
    C = (PADKEY + P - 1) // LO // P + 1
    KF = 2 * D // P
    KD = D // P
    KH = HID // P
    CW = D + W
    EPS = 1e-5

    BULK = 400
    FLIGHT = 8
    x_flat = x.rearrange("n d -> (n d)").rearrange("(c a w) -> c a w", c=BULK, a=16)
    x1_d = nc.dram_tensor("x1", (ROWS, D), fp32).ap()
    x1_head = x1_d[0:N, :].rearrange("n d -> (n d)").rearrange("(c a w) -> c a w", c=BULK, a=16)
    x1_flat = x1_d.rearrange("n d -> (n d)").rearrange("(c a w) -> c a w", c=BULK, a=16)
    out_flat = out.rearrange("n d -> (n d)").rearrange("(c a w) -> c a w", c=BULK, a=16)
    ZR = ROWS - N
    spare_rows = x1_d[N:ROWS, :].rearrange("(p a) d -> p (a d)", p=100)
    ROUNDS = BULK // FLIGHT
    PREP_ROUNDS = 16
    RING0 = 24
    RING1 = 18
    LEAD1 = RING1 + 2
    LAG = 4
    LAG1 = 6

    src_rows_d = nc.dram_tensor("src_rows", (T, P), fp32).ap()
    dst_rows_d = nc.dram_tensor("dst_rows", (T, P), fp32).ap()
    hi_rows_d = nc.dram_tensor("hi_rows", (2, T, P), fp16).ap()
    src_rows = src_rows_d.rearrange("(b j) p -> b (j p)", j=W)
    dst_rows = dst_rows_d.rearrange("(b j) p -> b (j p)", j=W)
    hi_rows = hi_rows_d.rearrange("k (b j) p -> b k (j p)", j=W)

    ctx = ExitStack()
    with ctx:
        def sb(name, shape, dt):
            return ctx.enter_context(nc.sbuf_tensor(name, shape, dt))

        def sem(name):
            return ctx.enter_context(nc.semaphore(name))

        keys = sb("keys", [P, 2, T], i32)
        row_idx = sb("row_idx", [P, T], i32)
        weight = sb("weight", [P, T], fp32)
        K_SRC, K_DST, K_SLO, K_DLO, K_VAL = range(5)
        per_edge = sb("per_edge", [P, NB, 5, W], fp32)
        degree = sb("degree", [P, NB, W], fp32)
        eps_col = sb("eps_col", [P, 1], fp32)
        ident = sb("ident", [P, P], fp32)
        hi_ident = sb("hi_ident", [P, C], fp32)
        lo_iota = sb("lo_iota", [P, LO], fp32)
        later = sb("later", [P, P], fp32)
        later_tile = sb("later_tile", [P, W, W], fp32)
        spare = sb("spare", [P, W], fp32)
        table = sb("table", [P, C, 2, LO], bf16)
        b1_col = sb("b1_col", [P, KH], fp32)
        b2_rows = sb("b2_rows", [P, 2, D], fp32)
        w1_hi = sb("w1_hi", [P, KF, HID], fp32r)
        w1_lo = sb("w1_lo", [P, KF, HID], fp32r)
        w2_hi = sb("w2_hi", [P, KH, D], fp32r)
        w2_lo = sb("w2_lo", [P, KH, D], fp32r)
        waited = sem("waited")

        bulk = [sem(f"bulk{k}") for k in range(FLIGHT)]
        bulk_out = [sem(f"bulk_out{k}") for k in range(FLIGHT)]

        with ExitStack() as stage:
            def sb(name, shape, dt):
                return stage.enter_context(nc.sbuf_tensor(name, shape, dt))

            def pb(name, shape, dt):
                return stage.enter_context(nc.psum_tensor(name, shape, dt))

            keys_f = sb("keys_f", [P, 2, T], fp32)
            hi_i = sb("hi_i", [P, 2, T], i32)
            lo_i = sb("lo_i", [P, 2, T], i32)
            hi_f = sb("hi_f", [P, 2, T], fp32)
            rows_f = sb("rows_f", [P, 2, 2, P], fp32)
            rows_h = sb("rows_h", [P, 2, 2, P], fp16)
            w1_f = sb("w1_f", [P, KF, HID], fp32)
            w2_f = sb("w2_f", [P, KH, D], fp32)
            wd = sb("wd", [P, KD, HID], fp32)
            b1_f = sb("b1_f", [KH, P], fp32)
            zero_rows = sb("zero_rows", [100, ZR * D // 100], fp32)
            zero_bf = sb("zero_bf", [P, 512], bf16)
            CH = C * P // 2
            count_iota_i = sb("count_iota_i", [P, CH], i32)
            count_iota = sb("count_iota", [P, CH], fp16)
            lo_iota_i = sb("lo_iota_i", [P, LO], i32)
            upper = sb("upper", [P, T], fp32)
            hi_in_half = sb("hi_in_half", [P, T], fp32)
            lo_and_half = sb("lo_and_half", [P, T], fp32)
            hi_ident_i = sb("hi_ident_i", [P, C], i32)
            part_i = sb("part_i", [P, W + 1], i32)
            part_f = sb("part_f", [P, W + 1], fp32)
            HOTS = 5
            RUN = 2 * HOTS
            assert T % RUN == 0
            hot_hi = sb("hot_hi", [P, HOTS, CH], bf16)
            hot_lo = sb("hot_lo", [P, HOTS, 2 * LO], bf16)
            node_count = sb("node_count", [P, C * P], fp32)
            table_i = sb("table_i", [P, C, LO], i32)
            table_r = sb("table_r", [P, C, LO], i32)
            table_rf = sb("table_rf", [P, C, LO], fp32)
            table_f = sb("table_f", [P, C, LO], fp32)
            ps_count = [pb(f"ps_count{h}", [P, 512], fp32) for h in range(2)]
            ps_tab = [pb(f"ps_tab{h}", [P, 512], fp32) for h in range(2)]
            ps_rows = [pb(f"ps_rows{h}", [P, 512], fp32) for h in range(2)]
            ps_b1 = pb("ps_b1", [P, 512], fp32)

            padded = sem("padded")
            consts = sem("consts")
            ident_zero = sem("ident_zero")
            edges_in = sem("edges_in")
            weights_in = sem("weights_in")
            split_keys = sem("split_keys")
            hots_ready = sem("hots_ready")
            hots_free = sem("hots_free")
            counted = sem("counted")
            copied = sem("copied")
            tabled = sem("tabled")
            tab_steps = sem("tab_steps")
            w_steps = sem("w_steps")
            rows_turned = sem("rows_turned")
            rows_copied = sem("rows_copied")
            rows_out = sem("rows_out")
            b1_turned = sem("b1_turned")
            zeroed = sem("zeroed")
            idents_made = sem("idents_made")

            block = stage.enter_context(nc.Block())

            @block.sync
            def _(sp):
                sp.wait_ge(padded, 3)
                sp.dma_start(keys[0:EP, 0, :], src.rearrange("(p t) -> p t", t=T)).then_inc(edges_in, 16)
                sp.dma_start(keys[0:EP, 1, :], dst.rearrange("(p t) -> p t", t=T)).then_inc(edges_in, 16)
                sp.dma_start(weight[0:EP, :], edge_weight.rearrange("(p t) -> p t", t=T)).then_inc(edges_in, 16)
                sp.dma_start(w1_f[:], w1.rearrange("(k p) h -> p k h", p=P)).then_inc(weights_in, 16)
                sp.dma_start(w2_f[:], w2.rearrange("(k p) d -> p k d", p=P)).then_inc(weights_in, 16)
                sp.dma_start(b1_f[:], b1.rearrange("(k p) -> k p", p=P)).then_inc(weights_in, 16)
                for a in range(G):
                    sp.dma_start(b2_rows[:, a, :], b2.partition_broadcast(P)).then_inc(weights_in, 16)
                sp.wait_ge(zeroed, 1)
                sp.dma_start(spare_rows, zero_rows[:]).then_inc(rows_out, 16)
                for k in range(FLIGHT):
                    sp.dma_start(x1_head[k], x_flat[k]).then_inc(bulk[k], 16)
                with sp.Fori(1, PREP_ROUNDS) as r:
                    for k in range(FLIGHT):
                        sp.wait_ge(bulk[k], 16 * r)
                        sp.dma_start(x1_head[bass.ds(FLIGHT * r + k, 1)],
                                     x_flat[bass.ds(FLIGHT * r + k, 1)]).then_inc(bulk[k], 16)

            @block.scalar
            def _(act):
                act.wait_ge(weights_in, 80)
                nc.scalar.activation(w1_hi[:, KD:KF, :], w1_f[:, KD:KF, :], ACT.Copy)
                nc.scalar.activation(w2_hi[:], w2_f[:], ACT.Copy)
                act.wait_ge(w_steps, 1)
                nc.scalar.activation(w1_hi[:, 0:KD, :], wd[:], ACT.Copy).then_inc(w_steps, 1)
                act.wait_ge(b1_turned, 1)
                nc.scalar.activation(b1_col[:], ps_b1[:, 0:KH], ACT.Copy)
                act.wait_ge(rows_copied, 2)
                for half, (t0, n) in enumerate(((0, P), (P, T - P))):
                    act.dma_start(src_rows_d[t0:t0 + n, :], rows_f[0:n, 0, half, :]).then_inc(rows_out, 16)
                    act.dma_start(dst_rows_d[t0:t0 + n, :], rows_f[0:n, 1, half, :]).then_inc(rows_out, 16)
                    for key in range(2):
                        act.dma_start(hi_rows_d[key, t0:t0 + n, :],
                                     rows_h[0:n, key, half, :]).then_inc(rows_out, 16)
                act.wait_ge(rows_out, 16 * 9)

            @block.gpsimd
            def _(pool):
                for key in range(2):
                    nc.gpsimd.iota(keys[:, key, :], [[0, T]], base=PADKEY, channel_multiplier=1).then_inc(padded, 1)
                nc.gpsimd.memset(weight[:], 0.0).then_inc(padded, 1)
                nc.gpsimd.memset(zero_rows[:], 0.0).then_inc(zeroed, 1)
                nc.gpsimd.memset(ident[:], 0.0).then_inc(ident_zero, 1)
                pool.wait_ge(ident_zero, 1)
                nc.gpsimd.affine_select(out=ident[:], in_=ident[:], compare_op=ALU.not_equal, fill=1.0,
                                        base=0, pattern=[[-1, P]], channel_multiplier=1).then_inc(idents_made, 1)
                nc.gpsimd.iota(count_iota_i[:], [[1, CH]], base=0, channel_multiplier=0).then_inc(consts, 1)
                nc.gpsimd.iota(lo_iota_i[:], [[1, LO]], base=0, channel_multiplier=0).then_inc(consts, 1)
                nc.gpsimd.iota(hi_ident_i[:], [[P, C]], base=0, channel_multiplier=1).then_inc(consts, 1)
                nc.gpsimd.iota(part_i[:, 0:W], [[P, W]], base=SPARE, channel_multiplier=1).then_inc(consts, 1)
                nc.gpsimd.iota(part_i[:, W:W + 1], [[0, 1]], base=0, channel_multiplier=1).then_inc(consts, 1)
                pool.wait_ge(weights_in, 80)
                nc.gpsimd.tensor_tensor(wd[:], w1_f[:, 0:KD, :], w1_f[:, KD:KF, :], ALU.subtract).then_inc(w_steps, 1)
                pool.wait_ge(w_steps, 2)
                nc.gpsimd.tensor_tensor(w1_lo[:, 0:KD, :], wd[:], w1_hi[:, 0:KD, :].bitcast(fp32), ALU.subtract)
                nc.gpsimd.tensor_tensor(w1_lo[:, KD:KF, :], w1_f[:, KD:KF, :],
                                        w1_hi[:, KD:KF, :].bitcast(fp32), ALU.subtract)
                nc.gpsimd.tensor_tensor(w2_lo[:], w2_f[:], w2_hi[:].bitcast(fp32), ALU.subtract)

            @block.vector
            def _(dve):
                nc.vector.memset(zero_bf[:], 0.0).then_inc(copied, 1)
                nc.vector.memset(eps_col[:], EPS)
                nc.vector.memset(later_tile[:], 0.0).then_inc(tab_steps, 1)
                dve.wait_ge(tab_steps, 1)
                for a in range(W - 1):
                    nc.vector.memset(later_tile[:, a, a + 1:W], 1.0)
                dve.wait_ge(consts, 5)
                nc.vector.tensor_copy(count_iota[:], count_iota_i[:])
                nc.vector.tensor_copy(lo_iota[:], lo_iota_i[:])
                nc.vector.tensor_copy(hi_ident[:], hi_ident_i[:])
                nc.vector.tensor_copy(part_f[:], part_i[:]).then_inc(tab_steps, 1)
                dve.wait_ge(tab_steps, 2)
                nc.vector.tensor_copy(spare[:], part_f[:, 0:W])
                nc.vector.tensor_scalar(later[:], lo_iota[:], part_f[:, W:W + 1], None, ALU.is_gt)
                dve.wait_ge(edges_in, 48)
                nc.vector.tensor_scalar(hi_i[:], keys[:], 7, None, ALU.logical_shift_right)
                nc.vector.tensor_scalar(lo_i[:], keys[:], LO - 1, None, ALU.bitwise_and)
                nc.vector.tensor_copy(keys_f[:], keys[:])
                nc.vector.tensor_scalar(row_idx[:], keys[:, 1, :], float(N - 1), None, ALU.min).then_inc(split_keys, 1)
                dve.wait_ge(split_keys, 1)
                nc.vector.tensor_copy(hi_f[:], hi_i[:]).then_inc(split_keys, 1)
                for kind, what in ((K_SRC, keys_f[:, 0, :]), (K_DST, keys_f[:, 1, :]), (K_SLO, lo_i[:, 0, :]),
                                   (K_DLO, lo_i[:, 1, :]), (K_VAL, weight[:])):
                    nc.vector.tensor_copy(per_edge[:, :, kind, :], what.rearrange("p (b j) -> p b j", j=W))\
                        .then_inc(split_keys, 1)
                dve.wait_ge(split_keys, 7)
                nc.vector.tensor_scalar(upper[:], hi_f[:, 1, :], float(CH), None, ALU.is_ge).then_inc(split_keys, 1)
                dve.wait_ge(split_keys, 8)
                nc.vector.scalar_tensor_tensor(hi_in_half[:], upper[:], float(-CH), hi_f[:, 1, :],
                                               ALU.mult, ALU.add).then_inc(split_keys, 1)
                nc.vector.scalar_tensor_tensor(lo_and_half[:].rearrange("p (b j) -> p b j", j=W),
                                               upper[:].rearrange("p (b j) -> p b j", j=W), float(LO),
                                               per_edge[:, :, K_DLO, :], ALU.mult, ALU.add).then_inc(split_keys, 1)
                dve.wait_ge(split_keys, 10)
                with dve.Fori(0, T // RUN) as r:
                    for j in range(RUN):
                        dve.wait_ge(hots_free, RUN * r + j + 1)
                        nc.vector.tensor_scalar(hot_lo[:, j % HOTS, :], count_iota[:, 0:2 * LO],
                                                lo_and_half[:, bass.ds(RUN * r + j, 1)], None, ALU.is_equal)
                        nc.vector.tensor_scalar(hot_hi[:, j % HOTS, :], count_iota[:], hi_in_half[:, bass.ds(RUN * r + j, 1)],
                                                None, ALU.is_equal).then_inc(hots_ready, 1)
                dve.wait_ge(rows_turned, 1)
                for h, n in enumerate((P, T - P)):
                    for key in range(2):
                        at = (2 * h + key) * P
                        nc.vector.tensor_copy(rows_f[0:n, key, h, :], ps_rows[0][0:n, at:at + P])
                        last = nc.vector.tensor_copy(rows_h[0:n, key, h, :], ps_rows[1][0:n, at:at + P])
                last.then_inc(rows_copied, 2)
                dve.wait_ge(counted, 1)
                for h in range(2):
                    last = nc.vector.tensor_copy(node_count[:, h * CH:(h + 1) * CH], ps_count[h][:, 0:CH])
                last.then_inc(copied, 1)
                dve.wait_ge(tabled, 1)
                for c in range(C):
                    last = nc.vector.tensor_copy(table_i[:, c, :], ps_tab[c // 4][:, (c % 4) * P:(c % 4 + 1) * P])
                last.then_inc(tab_steps, 1)
                dve.wait_ge(tab_steps, 3)
                nc.vector.tensor_scalar(table_r[:], table_i[:], 255, None, ALU.bitwise_and)
                nc.vector.tensor_copy(table_f[:], table_i[:]).then_inc(tab_steps, 1)
                dve.wait_ge(tab_steps, 4)
                nc.vector.tensor_copy(table_rf[:], table_r[:]).then_inc(tab_steps, 1)
                dve.wait_ge(tab_steps, 5)
                nc.vector.tensor_copy(table[:, :, 1, :], table_rf[:])
                nc.vector.tensor_tensor(table[:, :, 0, :], table_f[:], table_rf[:], ALU.subtract)

            @block.tensor
            def _(pe):
                pe.wait_ge(copied, 1)
                for h in range(2):
                    nc.tensor.matmul(ps_count[h][:, 0:CH], zero_bf[:, 0:P], zero_bf[:, 0:CH], start=True, stop=False)
                pe.sem_inc(hots_free, HOTS)
                with pe.Fori(0, T // RUN) as r:
                    for j in range(RUN):
                        pe.wait_ge(hots_ready, RUN * r + j + 1)
                        for h in range(2):
                            last = nc.tensor.matmul(ps_count[h][:, 0:CH], hot_lo[:, j % HOTS, h * LO:(h + 1) * LO],
                                                    hot_hi[:, j % HOTS, :], start=False, stop=False)
                        last.then_inc(hots_free, 1)
                for h in range(2):
                    last = nc.tensor.matmul(ps_count[h][:, 0:CH], zero_bf[:, 0:P], zero_bf[:, 0:CH],
                                            start=False, stop=True)
                last.then_inc(counted, 1)
                pe.wait_ge(idents_made, 1)
                for w, what in enumerate((keys_f, hi_f)):
                    for half, (t0, n) in enumerate(((0, P), (P, T - P))):
                        for key in range(2):
                            at = (2 * half + key) * P
                            last = nc.tensor.transpose(ps_rows[w][0:n, at:at + P], what[:, key, t0:t0 + n], ident[:])
                last.then_inc(rows_turned, 1)
                pe.wait_ge(weights_in, 80)
                nc.tensor.transpose(ps_b1[:, 0:KH], b1_f[:], ident[0:KH, 0:KH]).then_inc(b1_turned, 1)
                pe.wait_ge(copied, 2)
                for c in range(C):
                    last = nc.tensor.transpose(ps_tab[c // 4][:, (c % 4) * P:(c % 4 + 1) * P],
                                               node_count[:, c * P:(c + 1) * P], ident[:])
                last.then_inc(tabled, 1)

        with ExitStack() as stage:
            def sb(name, shape, dt):
                return stage.enter_context(nc.sbuf_tensor(name, shape, dt))

            def pb(name, shape, dt):
                return stage.enter_context(nc.psum_tensor(name, shape, dt))

            gather_idx = [sb(f"gather_idx{q}", [P, W], i32) for q in range(2)]
            rows = [sb(f"rows{q}", [P, W, D], fp32) for q in range(2)]
            src_row = [sb(f"src_row{q}", [P, W * P], fp32) for q in range(2)]
            hi_row = [sb(f"hi_row{q}", [P, 2, W * P], fp16) for q in range(2)]
            cols = [sb(f"cols{q}", [P, 5, W], fp32) for q in range(2)]
            moments = sb("moments", [P, W, 6], fp32)
            mean_var = [sb(f"mean_var{q}", [P, W, 2], fp32) for q in range(2)]
            std = sb("std", [P, W], fp32)
            rstd = [sb(f"rstd{q}", [P, W], fp32) for q in range(2)]
            shift = [sb(f"shift{q}", [P, W], fp32) for q in range(2)]
            normed = [sb(f"normed{q}", [P, W, D], fp32) for q in range(2)]
            hot = sb("hot", [P, C, 2, W * P], bf16)
            picked = sb("picked", [P, 2, W, LO], bf16)
            deg = [sb(f"deg{q}", [P, 2, W], fp32) for q in range(2)]
            deg_max = sb("deg_max", [P, W], fp32)
            deg_prod = sb("deg_prod", [P, W], fp32)
            root = sb("root", [P, W], fp32)
            inv_root = sb("inv_root", [P, W], fp32)
            coef = [sb(f"coef{q}", [P, W], fp32) for q in range(2)]
            same = sb("same", [P, W, W * P], fp32r)
            same_later = sb("same_later", [P, W, P], bf16)
            dup_in = [sb(f"dup_in{q}", [P, W], fp32) for q in range(2)]
            msg = sb("msg", [P, W, D], fp32)
            msg_hi = sb("msg_hi", [P, W, CW], fp32r)
            msg_lo = sb("msg_lo", [P, W, D], fp32r)
            sums_ring = sb("sums_ring", [P, RING0, W, CW], fp32)
            add_rows = [sb(f"add_rows{q}", [P, W, D], fp32) for q in range(2)]
            dup_tile = sb("dup_tile", [P, W, W], fp32)
            dup = sb("dup", [P, W], fp32)
            dup_all = sb("dup_all", [P, W], fp32)
            is_dup = sb("is_dup", [P, W], fp32)
            to_spare = sb("to_spare", [P, W], fp32)
            move = sb("move", [P, W], fp32)
            scatter_f = sb("scatter_f", [P, W], fp32)
            targets_all = sb("targets_all", [P, NB, W], i32)
            scatter_idx = [sb(f"scatter_idx{q}", [P, W], i32) for q in range(2)]
            ps_deg = [[pb(f"ps_deg{q}{k}", [P, W * P], fp32) for k in range(2)] for q in range(2)]
            ps_sum = [pb(f"ps_sum{a}", [P, 512], fp32) for a in range(W)]

            rows_in = [sem(f"rows_in{q}") for q in range(2)]
            src_row_in = [sem(f"src_row_in{q}") for q in range(2)]
            hi_row_in = [sem(f"hi_row_in{q}") for q in range(2)]
            add_rows_in = [sem(f"add_rows_in{q}") for q in range(2)]
            src_row_free = sem("src_row_free")
            idx_staged = sem("idx_staged")
            moments_done = sem("moments_done")
            var_done = sem("var_done")
            std_done = sem("std_done")
            rstd_done = sem("rstd_done")
            shift_done = sem("shift_done")
            normed_done = sem("normed_done")
            hot_ready = sem("hot_ready")
            deg_ready = sem("deg_ready")
            cols_ready = sem("cols_ready")
            same_ready = sem("same_ready")
            dup_in_done = sem("dup_in_done")
            deg_picked = sem("deg_picked")
            coef_steps = sem("coef_steps")
            root_done = sem("root_done")
            coef_ready = sem("coef_ready")
            msg_ready = sem("msg_ready")
            hi_ready = sem("hi_ready")
            lo_ready = sem("lo_ready")
            summed = sem("summed")
            in_ring = sem("in_ring")
            ring_free = sem("ring_free")
            add_rows_free = sem("add_rows_free")
            idx_steps = sem("idx_steps")
            idx_ready = sem("idx_ready")
            target_staged = sem("target_staged")
            scattered = sem("scattered")
            cnt_cols = sem("cnt_cols")

            block = stage.enter_context(nc.Block())

            @block.sync
            def _(sp):
                with sp.Fori(PREP_ROUNDS, ROUNDS) as r:
                    for k in range(FLIGHT):
                        sp.wait_ge(bulk[k], 16 * r)
                        sp.dma_start(x1_head[bass.ds(FLIGHT * r + k, 1)],
                                     x_flat[bass.ds(FLIGHT * r + k, 1)]).then_inc(bulk[k], 16)
                with sp.Fori(0, HALF) as t:
                    for q in range(2):
                        b = 2 * t + q
                        sp.wait_ge(in_ring, b + 1)
                        sp.wait_ge(add_rows_free, b + 1)
                        sp.sem_inc(waited, 1)
                        sp.dma_start(add_rows[q][:], sums_ring[:, bass.ds(b % RING0, 1), :, 0:D])\
                            .then_inc(add_rows_in[q], 16)

            @block.gpsimd
            def _(pool):
                nc.gpsimd.memset(msg_hi[:, :, D:CW].bitcast(fp32), 0.0).then_inc(cnt_cols, 1)
                pool.wait_ge(cnt_cols, 1)
                for j in range(W):
                    nc.gpsimd.memset(msg_hi[:, j, D + j:D + j + 1].bitcast(fp32), 1.0).then_inc(cnt_cols, 1)
                pool.sem_inc(add_rows_free, 2)
                pool.sem_inc(ring_free, RING0)

                def gather(b, q, half):
                    if half == 0:
                        pool.wait_ge(normed_done, b + 1)
                        pool.sem_inc(waited, 1)
                        nc.gpsimd.tensor_copy(gather_idx[q][:], row_idx[:, bass.ds(W * b, W)]).then_inc(idx_staged, 1)
                        pool.wait_ge(idx_staged, b + 1)
                        pool.sem_inc(waited, 1)
                    for j in range(half * W // 2, (half + 1) * W // 2):
                        pool.indirect_dma_start(
                            out=rows[q][:, j, :], out_offset=None, in_=x,
                            in_offset=bass.IndirectOffsetOnAxis(ap=gather_idx[q][:, j:j + 1], axis=0))\
                            .then_inc(rows_in[q], 16)

                def scatter(b, t, q):
                    pool.wait_ge(idx_ready, b + 1)
                    pool.sem_inc(waited, 1)
                    nc.gpsimd.tensor_copy(scatter_idx[q][:], targets_all[:, bass.ds(b, 1), :]).then_inc(target_staged, 1)
                    pool.wait_ge(target_staged, b + 1)
                    pool.wait_ge(add_rows_in[q], 16 * (t + 1))
                    pool.sem_inc(waited, 1)
                    for j in range(W):
                        pool.indirect_dma_start(
                            out=x1_d, out_offset=bass.IndirectOffsetOnAxis(ap=scatter_idx[q][:, j:j + 1], axis=0),
                            in_=add_rows[q][:, j, :], in_offset=None, compute_op=ALU.add)\
                            .then_inc(scattered, 16)

                def scatter_end(b):
                    pool.wait_ge(scattered, 16 * W * (b + 1))
                    pool.sem_inc(add_rows_free, 1)
                    pool.sem_inc(ring_free, 1)

                for b in range(2):
                    gather(b, b, 0)
                    gather(b, b, 1)
                with pool.Fori(1, RING0 // 2) as t:
                    for q in range(2):
                        gather(2 * t + q, q, 0)
                        gather(2 * t + q, q, 1)
                for k in range(FLIGHT):
                    pool.wait_ge(bulk[k], 16 * ROUNDS)
                FAST0 = (RING0 + 2 - LAG - 2) // 2
                with pool.Fori(0, FAST0) as n:
                    for u in range(4):
                        scatter(4 * n + u, 2 * n + u // 2, u % 2)
                        gather(2 * n + RING0 + u // 2, u // 2, u % 2)
                        scatter_end(4 * n + u)
                EVEN0 = NB - RING0 - 2 * FAST0
                with pool.Fori(0, EVEN0 // 2) as n:
                    for q in range(2):
                        scatter(2 * n + 4 * FAST0 + q, n + 2 * FAST0, q)
                        gather(2 * n + RING0 + 2 * FAST0 + q, q, 0)
                        gather(2 * n + RING0 + 2 * FAST0 + q, q, 1)
                        scatter_end(2 * n + 4 * FAST0 + q)
                for b in range(4 * FAST0 + EVEN0, NB):
                    scatter(b, b // 2, b % 2)
                    scatter_end(b)

            def following(b, t, q):
                return b + 1, t + q, 1 - q

            @block.vector
            def _(dve):
                dve.sem_inc(src_row_free, 2)

                def moments_of(b, t, q):
                    dve.wait_ge(rows_in[q], 16 * W * (t + 1))
                    for j in range(W):
                        last = nc.vector.bn_stats(moments[:, j, :], rows[q][:, j, :])
                    last.then_inc(moments_done, 1)

                def mean_var_of(b, t, q):
                    dve.wait_ge(moments_done, b + 1)
                    dve.sem_inc(waited, 1)
                    for j in range(W):
                        last = nc.vector.bn_aggr(mean_var[q][:, j, :], moments[:, j, :])
                    last.then_inc(var_done, 1)

                def hots_of(b, t, q):
                    dve.wait_ge(hi_row_in[q], 16 * (t + 1))
                    dve.wait_ge(deg_ready, b + 1)
                    for c in range(C):
                        last = nc.vector.tensor_scalar(hot[:, c, :, :], hi_row[q][:], hi_ident[:, c:c + 1],
                                                       None, ALU.is_equal)
                    last.then_inc(hot_ready, 1)

                def scales_of(b, t, q):
                    dve.wait_ge(std_done, b + 1)
                    nc.vector.reciprocal(rstd[q][:], std[:]).then_inc(rstd_done, 1)
                    dve.wait_ge(rstd_done, b + 1)
                    nc.vector.scalar_tensor_tensor(shift[q][:], mean_var[q][:, :, 0], -1.0, rstd[q][:],
                                                   ALU.mult, ALU.mult).then_inc(shift_done, 1)

                def degrees_of(b, t, q):
                    dve.wait_ge(cols_ready, b + 1)
                    dve.wait_ge(deg_ready, b + 2)
                    for k, kind in enumerate((K_SLO, K_DLO)):
                        for j in range(W):
                            last = nc.vector.scalar_tensor_tensor(
                                picked[:, k, j, :], lo_iota[:], cols[q][:, kind, j:j + 1],
                                ps_deg[q][k][:, j * P:(j + 1) * P], ALU.is_equal, ALU.mult,
                                accum_out=deg[q][:, k, j:j + 1])
                    last.then_inc(deg_picked, 1)
                    dve.wait_ge(deg_picked, b + 1)
                    nc.vector.tensor_scalar(deg_max[:], deg[q][:, 1, :], 1.0, None, ALU.max).then_inc(coef_steps, 1)
                    nc.vector.tensor_copy(degree[:, bass.ds(b, 1), :], deg[q][:, 1, :])
                    dve.wait_ge(coef_steps, 3 * b + 1)
                    nc.vector.scalar_tensor_tensor(deg_prod[:], deg[q][:, 0, :], 1.0, deg_max[:], ALU.max, ALU.mult)\
                        .then_inc(coef_steps, 1)

                def same_of(b, t, q):
                    dve.wait_ge(src_row_in[q], 16 * (t + 1))
                    dve.wait_ge(summed, b + 1)
                    for j in range(W):
                        last = nc.vector.tensor_scalar(same[:, j, :], src_row[q][:], cols[q][:, K_SRC, j:j + 1],
                                                       None, ALU.is_equal)
                    last.then_inc(same_ready, 1)

                def inv_root_of(b):
                    dve.wait_ge(root_done, b + 1)
                    nc.vector.reciprocal(inv_root[:], root[:]).then_inc(coef_steps, 1)

                def coef_of(b, q):
                    dve.wait_ge(coef_steps, 3 * b + 3)
                    nc.vector.tensor_tensor(coef[q][:], inv_root[:], cols[q][:, K_VAL, :], ALU.mult)\
                        .then_inc(coef_ready, 1)

                def later_of(b, q, j):
                    last = nc.vector.scalar_tensor_tensor(
                        same_later[:, j, :], src_row[q][:, j * P:(j + 1) * P], cols[q][:, K_SRC, j:j + 1],
                        later[:], ALU.is_equal, ALU.mult, accum_out=dup_in[q][:, j:j + 1])
                    if j == W - 1:
                        last.then_inc(dup_in_done, 1)

                def low_of(b, t, q):
                    dve.wait_ge(hi_ready, b + 1)
                    nc.vector.tensor_tensor(msg_lo[:], msg[:], msg_hi[:, :, 0:D].bitcast(fp32), ALU.subtract)\
                        .then_inc(lo_ready, 1)

                def dup_tiles_of(b, q):
                    dve.wait_ge(in_ring, b + 1)
                    nc.vector.tensor_tensor(dup_tile[:], sums_ring[:, bass.ds(b % RING0, 1), :, D:CW]
                                            .rearrange("p o j c -> p (o j) c"), later_tile[:], ALU.mult)\
                        .then_inc(idx_steps, 1)
                    nc.vector.tensor_tensor(to_spare[:], spare[:], cols[q][:, K_SRC, :], ALU.subtract)

                def dup_sum_of(b):
                    dve.wait_ge(idx_steps, 6 * b + 1)
                    nc.vector.tensor_reduce(dup[:], dup_tile[:], AX.X, ALU.add).then_inc(idx_steps, 1)

                def dup_all_of(b, q):
                    dve.wait_ge(idx_steps, 6 * b + 2)
                    nc.vector.tensor_tensor(dup_all[:], dup[:], dup_in[q][:], ALU.add).then_inc(idx_steps, 1)

                def is_dup_of(b):
                    dve.wait_ge(idx_steps, 6 * b + 3)
                    nc.vector.tensor_scalar(is_dup[:], dup_all[:], 0.5, None, ALU.is_gt).then_inc(idx_steps, 1)

                def move_of(b):
                    dve.wait_ge(idx_steps, 6 * b + 4)
                    nc.vector.tensor_tensor(move[:], is_dup[:], to_spare[:], ALU.mult).then_inc(idx_steps, 1)

                def target_of(b, q):
                    dve.wait_ge(idx_steps, 6 * b + 5)
                    nc.vector.tensor_tensor(scatter_f[:], move[:], cols[q][:, K_SRC, :], ALU.add).then_inc(idx_steps, 1)

                def keep_target(b):
                    dve.wait_ge(idx_steps, 6 * b + 6)
                    dve.sem_inc(waited, 1)
                    nc.vector.tensor_copy(targets_all[:, bass.ds(b, 1), :], scatter_f[:]).then_inc(idx_ready, 1)

                def columns_of(b, t, q):
                    nc.vector.tensor_copy(cols[q][:], per_edge[:, bass.ds(b, 1), :, :]).then_inc(cols_ready, 1)

                def step(b, t, q, first=False, last=False):
                    nxt = following(b, t, q)
                    if not last:
                        hots_of(*nxt)
                    degrees_of(b, t, q)
                    same_of(b, t, q)
                    inv_root_of(b)
                    if not first:
                        dup_tiles_of(b - 1, 1 - q)
                    coef_of(b, q)
                    if not first:
                        dup_sum_of(b - 1)
                    later_of(b, q, 0)
                    if not first:
                        dup_all_of(b - 1, 1 - q)
                    later_of(b, q, 1)
                    if not first:
                        is_dup_of(b - 1)
                    later_of(b, q, 2)
                    if not first:
                        move_of(b - 1)
                    later_of(b, q, 3)
                    if not first:
                        target_of(b - 1, 1 - q)
                    if not last:
                        moments_of(*nxt)
                    if not first:
                        keep_target(b - 1)
                    if not last:
                        mean_var_of(*nxt)
                        columns_of(*nxt)
                    dve.wait_ge(dup_in_done, b + 1)
                    dve.sem_inc(src_row_free, 1)
                    low_of(b, t, q)
                    if not last:
                        scales_of(*nxt)

                hots_of(0, 0, 0)
                moments_of(0, 0, 0)
                mean_var_of(0, 0, 0)
                columns_of(0, 0, 0)
                scales_of(0, 0, 0)
                step(0, 0, 0, first=True)
                with dve.Fori(0, HALF - 1) as i:
                    step(2 * i + 1, i, 1)
                    step(2 * i + 2, i + 1, 0)
                step(NB - 1, HALF - 1, 1, last=True)
                dup_tiles_of(NB - 1, 1)
                dup_sum_of(NB - 1)
                dup_all_of(NB - 1, 1)
                is_dup_of(NB - 1)
                move_of(NB - 1)
                target_of(NB - 1, 1)
                keep_target(NB - 1)

            @block.scalar
            def _(act):
                act.sem_inc(normed_done, 2)

                def load_hi(b, q):
                    if not (isinstance(b, int) and b < 2):
                        act.wait_ge(hot_ready, b - 1)
                    act.dma_start(hi_row[q][:], hi_rows[bass.ds(b, 1), :, :].partition_broadcast(P))\
                        .then_inc(hi_row_in[q], 16)

                def load_src(b, q):
                    act.wait_ge(src_row_free, b + 1)
                    act.dma_start(src_row[q][:], src_rows[bass.ds(b, 1), :].partition_broadcast(P))\
                        .then_inc(src_row_in[q], 16)

                def std_of(b, t, q):
                    act.wait_ge(var_done, b + 1)
                    if not (isinstance(b, int) and b == 0):
                        act.wait_ge(rstd_done, b)
                    nc.scalar.activation(std[:], mean_var[q][:, :, 1], ACT.Sqrt, bias=eps_col[:]).then_inc(std_done, 1)

                def norm(b, t, q):
                    act.wait_ge(shift_done, b + 1)
                    for j in range(W):
                        last = nc.scalar.activation(normed[q][:, j, :], rows[q][:, j, :], ACT.Relu,
                                                    bias=shift[q][:, j:j + 1], scale=rstd[q][:, j:j + 1])
                    last.then_inc(normed_done, 1)

                def root_of(b, t, q):
                    act.wait_ge(coef_steps, 3 * b + 2)
                    nc.scalar.activation(root[:], deg_prod[:], ACT.Sqrt).then_inc(root_done, 1)

                def message(b, t, q):
                    act.wait_ge(normed_done, b + 3)
                    act.wait_ge(coef_ready, b + 1)
                    act.wait_ge(summed, b + 1)
                    for j in range(W):
                        last = nc.scalar.activation(msg[:, j, :], normed[q][:, j, :], ACT.Copy,
                                                    scale=coef[q][:, j:j + 1])
                    last.then_inc(msg_ready, 1)
                    act.wait_ge(msg_ready, b + 1)
                    nc.scalar.activation(msg_hi[:, :, 0:D], msg[:], ACT.Copy).then_inc(hi_ready, 1)

                def to_ring(b, t, q):
                    act.wait_ge(summed, b + 2)
                    act.wait_ge(ring_free, b + 1)
                    act.sem_inc(waited, 1)
                    for j in range(W):
                        last = nc.scalar.activation(sums_ring[:, bass.ds(b % RING0, 1), j, :], ps_sum[j][:, 0:CW],
                                                    ACT.Copy)
                    last.then_inc(in_ring, 1)

                def step(b, t, q, first=False, last=False, load=True):
                    if load:
                        load_hi(b + 2, q)
                    root_of(b, t, q)
                    if not first:
                        to_ring(b - 1, t - 1 + q, 1 - q)
                    message(b, t, q)
                    if load:
                        load_src(b + 2, q)
                    if not last:
                        std_of(*following(b, t, q))
                        norm(*following(b, t, q))

                load_hi(0, 0)
                load_src(0, 0)
                load_hi(1, 1)
                load_src(1, 1)
                std_of(0, 0, 0)
                norm(0, 0, 0)
                step(0, 0, 0, first=True)
                with act.Fori(0, HALF - 2) as i:
                    step(2 * i + 1, i, 1)
                    step(2 * i + 2, i + 1, 0)
                step(NB - 3, HALF - 2, 1)
                step(NB - 2, HALF - 1, 0, load=False)
                step(NB - 1, HALF - 1, 1, last=True, load=False)
                to_ring(NB - 1, HALF - 1, 1)

            @block.tensor
            def _(pe):
                pe.sem_inc(deg_ready, 1)
                pe.sem_inc(summed, 1)
                pe.wait_ge(cnt_cols, 1 + W)

                def degrees(b, q):
                    pe.wait_ge(hot_ready, b + 1)
                    if not (isinstance(b, int) and b < 2):
                        pe.wait_ge(deg_picked, b - 1)
                    for k in range(2):
                        for j in range(W):
                            for c in range(C):
                                for part in range(2):
                                    last = nc.tensor.matmul(ps_deg[q][k][:, j * P:(j + 1) * P],
                                                            hot[:, c, k, j * P:(j + 1) * P], table[:, c, part, :],
                                                            start=(c == 0 and part == 0),
                                                            stop=(c == C - 1 and part == 1))
                    last.then_inc(deg_ready, 1)

                def sums(b):
                    pe.wait_ge(same_ready, b + 1)
                    pe.wait_ge(lo_ready, b + 1)
                    if not (isinstance(b, int) and b == 0):
                        pe.wait_ge(in_ring, b)
                    for a in range(W):
                        for j in range(W):
                            nc.tensor.matmul(ps_sum[a][:, 0:CW], same[:, j, a * P:(a + 1) * P], msg_hi[:, j, :],
                                             start=(j == 0), stop=False)
                        for j in range(W):
                            last = nc.tensor.matmul(ps_sum[a][:, 0:D], same[:, j, a * P:(a + 1) * P], msg_lo[:, j, :],
                                                    start=False, stop=(j == W - 1))
                    last.then_inc(summed, 1)

                degrees(0, 0)
                degrees(1, 1)
                sums(0)
                with pe.Fori(0, HALF - 1) as i:
                    degrees(2 * i + 2, 0)
                    sums(2 * i + 1)
                    degrees(2 * i + 3, 1)
                    sums(2 * i + 2)
                sums(NB - 1)

        with ExitStack() as stage:
            def sb(name, shape, dt):
                return stage.enter_context(nc.sbuf_tensor(name, shape, dt))

            def pb(name, shape, dt):
                return stage.enter_context(nc.psum_tensor(name, shape, dt))

            ends_idx = [sb(f"ends_idx{q}", [P, 2, W], i32) for q in range(2)]
            ends = [sb(f"ends{q}", [P, 2 * W, D], fp32) for q in range(2)]
            dst_row = [sb(f"dst_row{q}", [P, W * P], fp32) for q in range(2)]
            e_moments = sb("e_moments", [P, 2 * W, 6], fp32)
            e_mean_var = [sb(f"e_mean_var{q}", [P, 2 * W, 2], fp32) for q in range(2)]
            e_std = sb("e_std", [P, 2 * W], fp32)
            e_rstd = [sb(f"e_rstd{q}", [P, 2 * W], fp32) for q in range(2)]
            e_shift = [sb(f"e_shift{q}", [P, 2 * W], fp32) for q in range(2)]
            e_normed = sb("e_normed", [P, 2 * W, D], fp32)
            feat_hi = sb("feat_hi", [P, KF, W * P], fp32r)
            feat_lo = sb("feat_lo", [P, KF, W * P], fp32r)
            hid = [sb(f"hid{h}", [P, W * P], fp32) for h in range(2)]
            hid_hi = sb("hid_hi", [P, KH, W * P], fp32r)
            hid_lo = sb("hid_lo", [P, KH, W * P], fp32r)
            out_hi = sb("out_hi", [P, W, D], fp32r)
            out_lo = sb("out_lo", [P, W, D], fp32r)
            dst_col = [sb(f"dst_col{q}", [P, W], fp32) for q in range(2)]
            deg_col = [sb(f"deg_col{q}", [P, W], fp32) for q in range(2)]
            deg_eps = sb("deg_eps", [P, W], fp32)
            inv_deg = [sb(f"inv_deg{q}", [P, W], fp32) for q in range(2)]
            peers = [sb(f"peers{q}", [P, W, G * P], fp32r) for q in range(2)]
            after = sb("after", [P, G, G * P], bf16)
            peers_after = sb("peers_after", [P, W, G * P], bf16)
            n_after = sb("n_after", [P, W], fp32)
            e_is_dup = sb("e_is_dup", [P, W], fp32)
            e_to_spare = sb("e_to_spare", [P, W], fp32)
            e_move = sb("e_move", [P, W], fp32)
            e_target = sb("e_target", [P, W], fp32)
            e_targets_all = sb("e_targets_all", [P, NB, W], i32)
            target_idx = [sb(f"target_idx{q}", [P, W], i32) for q in range(2)]
            e_ring = sb("e_ring", [P, RING1, W, D], fp32)
            e_add_rows = [sb(f"e_add_rows{q}", [P, W, D], fp32) for q in range(2)]
            ps_t = [pb(f"ps_t{h}", [P, W * P], fp32) for h in range(2)]
            ps_h = [pb(f"ps_h{h}", [P, W * P], fp32) for h in range(2)]
            out_sum = [sb(f"out_sum{h}", [P, G * D], fp32) for h in range(2)]
            ps_m = [pb(f"ps_m{h}", [P, G * D], fp32) for h in range(2)]
            ps_s = [pb(f"ps_s{h}", [P, G * D], fp32) for h in range(2)]

            ends_in = [sem(f"ends_in{q}") for q in range(2)]
            dst_row_in = [sem(f"dst_row_in{q}") for q in range(2)]
            dst_row_free = sem("dst_row_free")
            ends_staged = sem("ends_staged")
            e_moments_done = sem("e_moments_done")
            e_var_done = sem("e_var_done")
            e_std_done = sem("e_std_done")
            e_rstd_done = sem("e_rstd_done")
            e_shift_done = sem("e_shift_done")
            e_normed_done = sem("e_normed_done")
            turned = sem("turned")
            feat_hi_done = sem("feat_hi_done")
            feat_lo_done = sem("feat_lo_done")
            mm1_done = sem("mm1_done")
            relu_done = sem("relu_done")
            hid_hi_done = sem("hid_hi_done")
            hid_lo_done = sem("hid_lo_done")
            mm2_done = sem("mm2_done")
            b2_added = sem("b2_added")
            out_hi_done = sem("out_hi_done")
            out_lo_done = sem("out_lo_done")
            e_cols_done = sem("e_cols_done")
            e_deg_done = sem("e_deg_done")
            inv_deg_done = sem("inv_deg_done")
            after_made = sem("after_made")
            peers_ready = sem("peers_ready")
            n_after_done = sem("n_after_done")
            e_idx_steps = sem("e_idx_steps")
            e_target_staged = sem("e_target_staged")
            e_target_ready = sem("e_target_ready")
            e_summed = sem("e_summed")
            e_in_ring = sem("e_in_ring")
            e_ring_free = sem("e_ring_free")
            e_add_in = [sem(f"e_add_in{q}") for q in range(2)]
            e_add_free = sem("e_add_free")
            e_scattered = sem("e_scattered")

            GROUPS = W // G
            block = stage.enter_context(nc.Block())

            def following(b, t, q):
                return b + 1, t + q, 1 - q

            def first(b):
                return isinstance(b, int) and b == 0

            @block.sync
            def _(sp):
                for k in range(FLIGHT):
                    sp.dma_start(out_flat[k], x1_flat[k]).then_inc(bulk_out[k], 16)
                with sp.Fori(1, ROUNDS) as r:
                    for k in range(FLIGHT):
                        sp.wait_ge(bulk_out[k], 16 * r)
                        sp.dma_start(out_flat[bass.ds(FLIGHT * r + k, 1)],
                                     x1_flat[bass.ds(FLIGHT * r + k, 1)]).then_inc(bulk_out[k], 16)
                with sp.Fori(0, HALF) as t:
                    for q in range(2):
                        b = 2 * t + q
                        sp.wait_ge(e_in_ring, GROUPS * (b + 2))
                        sp.sem_inc(waited, 1)
                        sp.wait_ge(e_add_free, b + 1)
                        sp.sem_inc(waited, 1)
                        sp.dma_start(e_add_rows[q][:], e_ring[:, bass.ds(b % RING1, 1), :, :])\
                            .then_inc(e_add_in[q], 16)

            @block.gpsimd
            def _(pool):
                pool.sem_inc(e_add_free, 2)
                pool.sem_inc(e_ring_free, RING1)

                def gather(b, q, end):
                    if end == 0:
                        pool.wait_ge(e_normed_done, b + 1)
                        pool.sem_inc(waited, 1)
                        nc.gpsimd.tensor_copy(ends_idx[q][:], keys[:, :, bass.ds(W * b, W)]).then_inc(ends_staged, 1)
                        pool.wait_ge(ends_staged, b + 1)
                        pool.sem_inc(waited, 1)
                    for j in range(W):
                        pool.indirect_dma_start(
                            out=ends[q][:, end * W + j, :], out_offset=None, in_=x1_d,
                            in_offset=bass.IndirectOffsetOnAxis(ap=ends_idx[q][:, 1 - end, j:j + 1], axis=0))\
                            .then_inc(ends_in[q], 16)

                def scatter(b, t, q, g):
                    if g == 0:
                        pool.wait_ge(e_target_ready, b + 1)
                        pool.sem_inc(waited, 1)
                        nc.gpsimd.tensor_copy(target_idx[q][:], e_targets_all[:, bass.ds(b, 1), :])\
                            .then_inc(e_target_staged, 1)
                        pool.wait_ge(e_target_staged, b + 1)
                        pool.wait_ge(e_add_in[q], 16 * (t + 1))
                        pool.sem_inc(waited, 1)
                    for j in range(G * g, G * g + G):
                        pool.indirect_dma_start(
                            out=out, out_offset=bass.IndirectOffsetOnAxis(ap=target_idx[q][:, j:j + 1], axis=0),
                            in_=e_add_rows[q][:, j, :], in_offset=None, compute_op=ALU.add)\
                            .then_inc(e_scattered, 16)

                def scatter_end(b, g):
                    pool.wait_ge(e_scattered, 16 * G * (GROUPS * b + g + 1))
                    pool.sem_inc(waited, 1)
                    if g == GROUPS - 1:
                        pool.sem_inc(e_add_free, 1)
                        pool.sem_inc(e_ring_free, 1)

                for b in range(2):
                    gather(b, b, 0)
                    gather(b, b, 1)
                with pool.Fori(1, LEAD1 // 2) as t:
                    for q in range(2):
                        gather(2 * t + q, q, 0)
                        gather(2 * t + q, q, 1)
                for k in range(FLIGHT):
                    pool.wait_ge(bulk_out[k], 16 * ROUNDS)
                FAST1 = min((LEAD1 - LAG1) // 2, (NB - LEAD1) // 4)
                with pool.Fori(0, FAST1) as n:
                    for u in range(6):
                        for g in range(GROUPS):
                            scatter(6 * n + u, 3 * n + u // 2, u % 2, g)
                            slot = GROUPS * u + g
                            if slot % 3 != 2:
                                half = slot // 3 * 2 + slot % 3
                                gather(4 * n + LEAD1 + half // 2, half // 2 % 2, half % 2)
                            scatter_end(6 * n + u, g)
                EVEN1 = NB - LEAD1 - 4 * FAST1
                if EVEN1:
                    with pool.Fori(0, EVEN1 // 2) as n:
                        for q in range(2):
                            for g in range(GROUPS):
                                scatter(2 * n + 6 * FAST1 + q, n + 3 * FAST1, q, g)
                                gather(2 * n + LEAD1 + 4 * FAST1 + q, q, g)
                                scatter_end(2 * n + 6 * FAST1 + q, g)
                for b in range(6 * FAST1 + EVEN1, NB):
                    for g in range(GROUPS):
                        scatter(b, b // 2, b % 2, g)
                        scatter_end(b, g)

            @block.vector
            def _(dve):
                dve.sem_inc(dst_row_free, 2)
                nc.vector.memset(after[:], 0.0).then_inc(after_made, 1)
                dve.wait_ge(after_made, 1)
                nc.vector.memset(after[:, 0, P:G * P], 1.0)
                nc.vector.tensor_copy(after[:, 0, 0:P], later[:])
                nc.vector.tensor_copy(after[:, 1, P:G * P], later[:]).then_inc(after_made, 1)
                dve.wait_ge(after_made, 2)

                def moments_of(b, t, q, part):
                    if part == 0:
                        dve.wait_ge(ends_in[q], 16 * 2 * W * (t + 1))
                    for r in range(part * W, (part + 1) * W):
                        last = nc.vector.bn_stats(e_moments[:, r, :], ends[q][:, r, :])
                    if part == 1:
                        last.then_inc(e_moments_done, 1)

                def mean_var_of(b, t, q):
                    dve.wait_ge(e_moments_done, b + 1)
                    dve.sem_inc(waited, 1)
                    for r in range(2 * W):
                        last = nc.vector.bn_aggr(e_mean_var[q][:, r, :], e_moments[:, r, :])
                    last.then_inc(e_var_done, 1)

                def scales_of(b, t, q):
                    dve.wait_ge(e_std_done, b + 1)
                    nc.vector.reciprocal(e_rstd[q][:], e_std[:]).then_inc(e_rstd_done, 1)
                    dve.wait_ge(e_rstd_done, b + 1)
                    nc.vector.scalar_tensor_tensor(e_shift[q][:], e_mean_var[q][:, :, 0], -1.0, e_rstd[q][:],
                                                   ALU.mult, ALU.mult).then_inc(e_shift_done, 1)

                def peers_of(b, t, q):
                    nc.vector.tensor_copy(dst_col[q][:], per_edge[:, bass.ds(b, 1), K_DST, :])
                    nc.vector.tensor_copy(deg_col[q][:], degree[:, bass.ds(b, 1), :]).then_inc(e_cols_done, 1)
                    dve.wait_ge(e_cols_done, b + 1)
                    nc.vector.tensor_scalar(deg_eps[:], deg_col[q][:], 1e-8, None, ALU.add).then_inc(e_deg_done, 1)
                    dve.wait_ge(dst_row_in[q], 16 * (t + 1))
                    dve.wait_ge(e_summed, GROUPS * b)
                    for j in range(W):
                        g = j // G
                        last = nc.vector.tensor_scalar(peers[q][:, j, :], dst_row[q][:, g * G * P:(g + 1) * G * P],
                                                       dst_col[q][:, j:j + 1], None, ALU.is_equal)
                    last.then_inc(peers_ready, 1)

                def after_of(b, t, q):
                    for j in range(W):
                        g = j // G
                        last = nc.vector.scalar_tensor_tensor(
                            peers_after[:, j, :], dst_row[q][:, g * G * P:(g + 1) * G * P], dst_col[q][:, j:j + 1],
                            after[:, j % G, :], ALU.is_equal, ALU.mult, accum_out=n_after[:, j:j + 1])
                    last.then_inc(n_after_done, 1)
                    dve.wait_ge(e_deg_done, b + 1)
                    dve.wait_ge(e_in_ring, GROUPS * b)
                    nc.vector.reciprocal(inv_deg[q][:], deg_eps[:]).then_inc(inv_deg_done, 1)
                    nc.vector.tensor_tensor(e_to_spare[:], spare[:], dst_col[q][:], ALU.subtract)

                def targets_of(b, t, q):
                    dve.wait_ge(n_after_done, b + 1)
                    dve.sem_inc(dst_row_free, 1)
                    nc.vector.tensor_scalar(e_is_dup[:], n_after[:], 0.5, None, ALU.is_gt).then_inc(e_idx_steps, 1)
                    dve.wait_ge(e_idx_steps, 3 * b + 1)
                    nc.vector.tensor_tensor(e_move[:], e_is_dup[:], e_to_spare[:], ALU.mult).then_inc(e_idx_steps, 1)
                    dve.wait_ge(e_idx_steps, 3 * b + 2)
                    nc.vector.tensor_tensor(e_target[:], e_move[:], dst_col[q][:], ALU.add).then_inc(e_idx_steps, 1)
                    dve.wait_ge(e_idx_steps, 3 * b + 3)
                    dve.sem_inc(waited, 1)
                    nc.vector.tensor_copy(e_targets_all[:, bass.ds(b, 1), :], e_target[:]).then_inc(e_target_ready, 1)

                def hid_low(b, m):
                    dve.wait_ge(hid_hi_done, KH * b + m + 1)
                    nc.vector.tensor_tensor(hid_lo[:, m, :], hid[m % 2][:], hid_hi[:, m, :].bitcast(fp32),
                                            ALU.subtract).then_inc(hid_lo_done, 1)

                def feat_low(b, k):
                    dve.wait_ge(feat_hi_done, KF * b + k + 1)
                    nc.vector.tensor_tensor(feat_lo[:, k, :], ps_t[k % 2][:], feat_hi[:, k, :].bitcast(fp32),
                                            ALU.subtract).then_inc(feat_lo_done, 1)

                def add_b2(b, g):
                    dve.wait_ge(mm2_done, GROUPS * b + g + 1)
                    nc.vector.tensor_tensor(out_sum[g][:], ps_m[g][:], b2_rows[:].rearrange("p a d -> p (a d)"),
                                            ALU.add).then_inc(b2_added, 1)

                def out_low(b, g):
                    dve.wait_ge(out_hi_done, GROUPS * b + g + 1)
                    nc.vector.tensor_tensor(out_lo[:, G * g:G * g + G, :].rearrange("p a d -> p (a d)"), out_sum[g][:],
                                            out_hi[:, G * g:G * g + G, :].rearrange("p a d -> p (a d)").bitcast(fp32),
                                            ALU.subtract).then_inc(out_lo_done, 1)

                def step(b, t, q, last=False, second=True):
                    if not last:
                        scales_of(*following(b, t, q))
                    hid_low(b, 0)
                    peers_of(b, t, q)
                    hid_low(b, 1)
                    after_of(b, t, q)
                    hid_low(b, 2)
                    targets_of(b, t, q)
                    hid_low(b, 3)
                    if not last:
                        feat_low(b + 1, 0)
                        feat_low(b + 1, 1)
                    if second:
                        moments_of(b + 2, t + 1, q, 0)
                    add_b2(b, 0)
                    if not last:
                        feat_low(b + 1, 2)
                        feat_low(b + 1, 3)
                    out_low(b, 0)
                    if second:
                        moments_of(b + 2, t + 1, q, 1)
                    add_b2(b, 1)
                    if second:
                        mean_var_of(b + 2, t + 1, q)
                    out_low(b, 1)

                for b in range(2):
                    moments_of(b, 0, b, 0)
                    moments_of(b, 0, b, 1)
                    mean_var_of(b, 0, b)
                    if b == 0:
                        scales_of(0, 0, 0)
                for k in range(KF):
                    feat_low(0, k)
                step(0, 0, 0)
                with dve.Fori(0, HALF - 2) as i:
                    step(2 * i + 1, i, 1)
                    step(2 * i + 2, i + 1, 0)
                step(NB - 3, HALF - 2, 1)
                step(NB - 2, HALF - 1, 0, second=False)
                step(NB - 1, HALF - 1, 1, last=True, second=False)

            @block.scalar
            def _(act):
                act.sem_inc(e_normed_done, 2)
                act.sem_inc(e_in_ring, GROUPS)

                def load_keys(b, q):
                    act.wait_ge(dst_row_free, b + 1)
                    act.dma_start(dst_row[q][:], dst_rows[bass.ds(b, 1), :].partition_broadcast(P))\
                        .then_inc(dst_row_in[q], 16)

                def std_of(b, t, q):
                    act.wait_ge(e_var_done, b + 1)
                    if not first(b):
                        act.wait_ge(e_rstd_done, b)
                    nc.scalar.activation(e_std[:], e_mean_var[q][:, :, 1], ACT.Sqrt, bias=eps_col[:])\
                        .then_inc(e_std_done, 1)

                def norm(b, t, q, r0, r1):
                    if r0 == 0:
                        act.wait_ge(e_shift_done, b + 1)
                        if not first(b):
                            act.wait_ge(turned, KF * b)
                    for r in range(r0, r1):
                        last = nc.scalar.activation(e_normed[:, r, :], ends[q][:, r, :], ACT.Relu,
                                                    bias=e_shift[q][:, r:r + 1], scale=e_rstd[q][:, r:r + 1])
                    if r1 == 2 * W:
                        last.then_inc(e_normed_done, 1)

                def feat_high(b, k):
                    act.wait_ge(turned, KF * b + k + 1)
                    nc.scalar.activation(feat_hi[:, k, :], ps_t[k % 2][:], ACT.Copy).then_inc(feat_hi_done, 1)

                def hid_high(b, m):
                    act.wait_ge(mm1_done, KH * b + m + 1)
                    if not (first(b) and m < 2):
                        act.wait_ge(hid_lo_done, KH * b + m - 1)
                    nc.scalar.activation(hid[m % 2][:], ps_h[m % 2][:], ACT.Relu, bias=b1_col[:, m:m + 1])\
                        .then_inc(relu_done, 1)
                    act.wait_ge(relu_done, KH * b + m + 1)
                    nc.scalar.activation(hid_hi[:, m, :], hid[m % 2][:], ACT.Copy).then_inc(hid_hi_done, 1)

                def out_high(b, g):
                    act.wait_ge(b2_added, GROUPS * b + g + 1)
                    nc.scalar.activation(out_hi[:, G * g:G * g + G, :].rearrange("p a d -> p (a d)"), out_sum[g][:],
                                         ACT.Copy).then_inc(out_hi_done, 1)

                def scale(b, q, g):
                    act.wait_ge(e_summed, GROUPS * (b + 1) + g + 1)
                    act.wait_ge(e_ring_free, b + 1)
                    act.wait_ge(inv_deg_done, b + 1)
                    act.sem_inc(waited, 1)
                    for a in range(G):
                        j = G * g + a
                        last = nc.scalar.activation(e_ring[:, bass.ds(b % RING1, 1), j, :], ps_s[g][:, a * D:(a + 1) * D],
                                                    ACT.Copy, scale=inv_deg[q][:, j:j + 1])
                    last.then_inc(e_in_ring, 1)

                def step(b, t, q, last=False, load=True):
                    nxt = following(b, t, q)
                    if not last:
                        std_of(*nxt)
                    hid_high(b, 0)
                    if not last:
                        norm(*nxt, 0, 3)
                    hid_high(b, 1)
                    if not last:
                        norm(*nxt, 3, 6)
                    hid_high(b, 2)
                    if not last:
                        norm(*nxt, 6, 8)
                    hid_high(b, 3)
                    for g in range(GROUPS):
                        if not last:
                            feat_high(b + 1, 2 * g)
                            feat_high(b + 1, 2 * g + 1)
                        if not first(b):
                            scale(b - 1, 1 - q, g)
                        out_high(b, g)
                    if load:
                        load_keys(b + 2, q)

                load_keys(0, 0)
                load_keys(1, 1)
                std_of(0, 0, 0)
                norm(0, 0, 0, 0, 2 * W)
                for k in range(KF):
                    feat_high(0, k)
                step(0, 0, 0)
                with act.Fori(0, HALF - 2) as i:
                    step(2 * i + 1, i, 1)
                    step(2 * i + 2, i + 1, 0)
                step(NB - 3, HALF - 2, 1)
                step(NB - 2, HALF - 1, 0, load=False)
                step(NB - 1, HALF - 1, 1, last=True, load=False)
                for g in range(GROUPS):
                    scale(NB - 1, 1, g)

            @block.tensor
            def _(pe):
                pe.sem_inc(e_summed, GROUPS)

                def turn(b, k):
                    if k == 0:
                        pe.wait_ge(e_normed_done, b + 3)
                    if not (first(b) and k < 2):
                        pe.wait_ge(feat_lo_done, KF * b + k - 1)
                    end, c = k // KD, k % KD
                    for j in range(W):
                        last = nc.tensor.transpose(ps_t[k % 2][:, j * P:(j + 1) * P],
                                                   e_normed[:, end * W + j, c * P:(c + 1) * P], ident[:])
                    last.then_inc(turned, 1)

                def mlp_in(b):
                    for m in range(KH):
                        if not (first(b) and m < 2):
                            pe.wait_ge(relu_done, KH * b + m - 1)
                        for k in range(KF):
                            if m == 0:
                                pe.wait_ge(feat_lo_done, KF * b + k + 1)
                            for n, (w, f) in enumerate(((w1_hi, feat_hi), (w1_hi, feat_lo), (w1_lo, feat_hi))):
                                last = nc.tensor.matmul(ps_h[m % 2][:], w[:, k, m * P:(m + 1) * P], f[:, k, :],
                                                        start=(k == 0 and n == 0), stop=(k == KF - 1 and n == 2))
                        last.then_inc(mm1_done, 1)

                def mlp_out(b, g):
                    if g == 0:
                        pe.wait_ge(hid_lo_done, KH * (b + 1))
                    if not first(b):
                        pe.wait_ge(b2_added, GROUPS * (b - 1) + g + 1)
                    for a in range(G):
                        at = (G * g + a) * P
                        for m in range(KH):
                            for n, (h, w) in enumerate(((hid_hi, w2_hi), (hid_hi, w2_lo), (hid_lo, w2_hi))):
                                last = nc.tensor.matmul(ps_m[g][:, a * D:(a + 1) * D], h[:, m, at:at + P], w[:, m, :],
                                                        start=(m == 0 and n == 0), stop=(m == KH - 1 and n == 2))
                    last.then_inc(mm2_done, 1)

                def sums(b, q):
                    pe.wait_ge(peers_ready, b + 1)
                    for g in range(GROUPS):
                        pe.wait_ge(out_lo_done, GROUPS * b + g + 1)
                        pe.wait_ge(e_in_ring, GROUPS * b + g + 1)
                        for a in range(G):
                            for n, part in enumerate((out_hi, out_lo)):
                                for j in range(G * g, G * g + G):
                                    last = nc.tensor.matmul(ps_s[g][:, a * D:(a + 1) * D],
                                                            peers[q][:, j, a * P:(a + 1) * P], part[:, j, :],
                                                            start=(n == 0 and j == G * g),
                                                            stop=(n == 1 and j == G * g + G - 1))
                        last.then_inc(e_summed, 1)

                def step(b, t, q, last=False):
                    mlp_in(b)
                    if not first(b):
                        sums(b - 1, 1 - q)
                    for g in range(GROUPS):
                        if not last:
                            turn(b + 1, 2 * g)
                            turn(b + 1, 2 * g + 1)
                        mlp_out(b, g)

                for k in range(KF):
                    turn(0, k)
                step(0, 0, 0)
                with pe.Fori(0, HALF - 1) as i:
                    step(2 * i + 1, i, 1)
                    step(2 * i + 2, i + 1, 0)
                step(NB - 1, HALF - 1, 1, last=True)
                sums(NB - 1, 1)


_OUT_SPARE = 800


def kernel(**inputs):
    import numpy as _np
    import concourse.bacc as _bacc
    from concourse import mybir as _mybir
    from concourse.bass_utils import run_bass_kernel_spmd as _run

    nc = _bacc.Bacc("TRN2", target_bir_lowering=False, num_devices=1)
    arrays, args = {}, []
    for name in ("x", "src", "dst", "edge_weight", "L1_gnn_W1", "L1_gnn_b1", "L1_gnn_W2", "L1_gnn_b2"):
        a = _np.ascontiguousarray(inputs[name])
        arrays[f"in_{name}"] = a
        args.append(nc.dram_tensor(f"in_{name}", a.shape, _mybir.dt.from_np(a.dtype), kind="ExternalInput").ap())
    nodes, width = inputs["x"].shape
    out = nc.dram_tensor("table_out", (nodes + _OUT_SPARE, width), _mybir.dt.float32, kind="ExternalOutput").ap()
    gnn_preln_two_layers(nc, *args, out)
    r = _run(nc, [arrays], core_ids=[0])
    return r.results[0]["table_out"][:nodes]
```
